# Optimizing a Trainium2 kernel written in Bass

```python
import numpy as np
import jax
import jax.numpy as jnp

def _softmax(x, axis=-1):
    return jax.nn.softmax(x, axis=axis)

def _gelu(x):
    return jax.nn.gelu(x, approximate=True)

def _silu(x):
    return jax.nn.silu(x)

def _sigmoid(x):
    return jax.nn.sigmoid(x)

def _layernorm(x, axis=-1, eps=1e-05):
    m = jnp.mean(x, axis=axis, keepdims=True)
    v = jnp.var(x, axis=axis, keepdims=True)
    return (x - m) / jnp.sqrt(v + eps)

def _scatter_add(tgt, idx, src, axis=0):
    return tgt.at[idx].add(src)

def _segment_sum(src, seg, n):
    return jax.ops.segment_sum(src, seg, n)
kernel_name = 'mk_decoder_postln_d1_seqx_r4_0e3bf9'

def setup_inputs(seed: int=0):
    np.random.seed(seed)
    _w = jnp.asarray

    def _rec_inputs():
        import jax
        import jax.numpy as jnp
        _rk = jax.random.key(seed)
        x = 7.22e-05 + 1 * jax.random.normal(jax.random.fold_in(_rk, 1), (8, 112, 512), jnp.float32)
        _lenS = 112 - jax.random.randint(jax.random.fold_in(_rk, 7), (8,), 0, max(1, 112 // 4) + 1, jnp.int32)
        _lenS2 = 375 - jax.random.randint(jax.random.fold_in(_rk, 8), (8,), 0, max(1, 375 // 4) + 1, jnp.int32)
        _ctx_512P = jax.random.normal(jax.random.fold_in(_rk, 11), (8, 16, 128), jnp.float32)
        _ctx_512c = jax.random.dirichlet(jax.random.fold_in(_rk, 511), 0.3 * jnp.ones((16,), jnp.float32), (8, 375))
        _ctx_512t = jnp.einsum('bsk,bkd->bsd', _ctx_512c, _ctx_512P)
        _ctx_512t = _ctx_512t * jax.lax.rsqrt(jnp.mean(jnp.square(_ctx_512t)) + 1e-12) * 0.953939
        ctx_512 = -0.000514642 + 1.00011 * (_ctx_512t + 0.3 * jax.random.normal(jax.random.fold_in(_rk, 611), (8, 375, 128), jnp.float32))
        return (x, ctx_512)
    x, ctx_512 = _rec_inputs()

    def _L0_attn_setup():
        import jax, jax.numpy as jnp
        import numpy as np
        import math
        DIM = 512
        NH = 16
        Q_RANK = 384
        KV_RANK = 128
        D_NOPE = 128
        D_ROPE = 64
        D_V = 128
        EPS = 1e-06
        B, S = (2, 512)
        THETA = 10000.0

        def _rms_norm(x, w):
            return x * jax.lax.rsqrt(jnp.mean(x * x, axis=-1, keepdims=True) + EPS) * w

        def _rope_cos_sin(seq_len, d):
            inv_freq = 1.0 / THETA ** (jnp.arange(0, d, 2, dtype=jnp.float32) / d)
            t = jnp.arange(seq_len, dtype=jnp.float32)
            freqs = jnp.outer(t, inv_freq)
            return (jnp.cos(freqs), jnp.sin(freqs))

        def _apply_rope(x, cos, sin):
            x1 = x[..., 0::2]
            x2 = x[..., 1::2]
            c = cos[None, :, None, :]
            s = sin[None, :, None, :]
            o1 = x1 * c - x2 * s
            o2 = x1 * s + x2 * c
            return jnp.stack([o1, o2], axis=-1).reshape(x.shape)
        if __name__ == '__main__':
            inp = setup_inputs()
            y = jax.jit(reference)(**inp)
            print(y.shape, y.dtype)
        key = jax.random.key(seed)
        ks = jax.random.split(key, 10)
        sd = 0.02
        return {'x': jax.random.normal(ks[0], (B, S, DIM), dtype=jnp.float32), 'wq_down': jax.random.normal(ks[1], (Q_RANK, DIM), dtype=jnp.float32) * sd, 'wq_up': jax.random.normal(ks[2], (NH * D_NOPE, Q_RANK), dtype=jnp.float32) * sd, 'wq_rope': jax.random.normal(ks[3], (NH * D_ROPE, Q_RANK), dtype=jnp.float32) * sd, 'q_norm_w': jnp.ones((Q_RANK,), dtype=jnp.float32), 'wkv_down': jax.random.normal(ks[4], (KV_RANK, DIM), dtype=jnp.float32) * sd, 'kv_norm_w': jnp.ones((KV_RANK,), dtype=jnp.float32), 'wkv_up': jax.random.normal(ks[5], (NH * (D_NOPE + D_V), KV_RANK), dtype=jnp.float32) * sd, 'wk_rope': jax.random.normal(ks[6], (D_ROPE, DIM), dtype=jnp.float32) * sd, 'wo': jax.random.normal(ks[7], (DIM, NH * D_V), dtype=jnp.float32) * sd}
    _L0_attn_all = _L0_attn_setup()
    _L0_attn_in = {k: v for k, v in _L0_attn_all.items() if k in ('wq_down', 'wq_up', 'wq_rope', 'q_norm_w', 'wkv_down', 'kv_norm_w', 'wkv_up', 'wk_rope', 'wo')}
    del _L0_attn_all

    def _L0_xattn_setup():
        import jax, jax.numpy as jnp
        import numpy as np
        B, S, H, NH, L = (2, 512, 512, 16, 128)
        HD = H // NH
        key = jax.random.key(seed)
        k1, k2, k3, k4, k5 = jax.random.split(key, 5)
        scale = 0.02
        return {'q': jax.random.normal(k1, (B, S, H), dtype=jnp.float32), 'latent_kv': jax.random.normal(k2, (B, S, L), dtype=jnp.float32), 'Wq': jax.random.normal(k3, (H, H), dtype=jnp.float32) * scale, 'Wkv_expand': jax.random.normal(k4, (2 * H, L), dtype=jnp.float32) * scale, 'Wout': jax.random.normal(k5, (H, H), dtype=jnp.float32) * scale}
    _L0_xattn_all = _L0_xattn_setup()
    _L0_xattn_in = {k: v for k, v in _L0_xattn_all.items() if k in ('Wq', 'Wkv_expand', 'Wout')}
    del _L0_xattn_all

    def _L0_ffn_setup():
        import jax, jax.numpy as jnp
        import numpy as np
        D = 512
        E = 16
        TOP_K = 2
        S_EXP = 2
        H_R = D // E * 4
        H_S = D * 4
        B, S = (4, 512)
        key = jax.random.key(seed)
        ks = jax.random.split(key, 12)
        sc = 0.02
        return {'x': jax.random.normal(ks[0], (B, S, D), jnp.float32), 'gate_w': jax.random.normal(ks[1], (D, E), jnp.float32) * sc, 'gate_b': jnp.zeros((E,), jnp.float32), 'ew1': jax.random.normal(ks[2], (E, D, H_R), jnp.float32) * sc, 'eb1': jnp.zeros((E, H_R), jnp.float32), 'ew2': jax.random.normal(ks[3], (E, H_R, D), jnp.float32) * sc, 'eb2': jnp.zeros((E, D), jnp.float32), 'sw1': jax.random.normal(ks[4], (S_EXP, D, H_S), jnp.float32) * sc, 'sb1': jnp.zeros((S_EXP, H_S), jnp.float32), 'sw2': jax.random.normal(ks[5], (S_EXP, H_S, D), jnp.float32) * sc, 'sb2': jnp.zeros((S_EXP, D), jnp.float32)}
    _L0_ffn_all = _L0_ffn_setup()
    _L0_ffn_in = {k: v for k, v in _L0_ffn_all.items() if k in ('gate_w', 'gate_b', 'ew1', 'eb1', 'ew2', 'eb2', 'sw1', 'sb1', 'sw2', 'sb2')}
    del _L0_ffn_all
    return {'x': x, 'ctx_512': ctx_512, 'L0_attn_wq_down': _L0_attn_in['wq_down'], 'L0_attn_wq_up': _L0_attn_in['wq_up'], 'L0_attn_wq_rope': _L0_attn_in['wq_rope'], 'L0_attn_q_norm_w': _L0_attn_in['q_norm_w'], 'L0_attn_wkv_down': _L0_attn_in['wkv_down'], 'L0_attn_kv_norm_w': _L0_attn_in['kv_norm_w'], 'L0_attn_wkv_up': _L0_attn_in['wkv_up'], 'L0_attn_wk_rope': _L0_attn_in['wk_rope'], 'L0_attn_wo': _L0_attn_in['wo'], 'L0_xattn_Wq': _L0_xattn_in['Wq'], 'L0_xattn_Wkv_expand': _L0_xattn_in['Wkv_expand'], 'L0_xattn_Wout': _L0_xattn_in['Wout'], 'L0_ffn_gate_w': _L0_ffn_in['gate_w'], 'L0_ffn_gate_b': _L0_ffn_in['gate_b'], 'L0_ffn_ew1': _L0_ffn_in['ew1'], 'L0_ffn_eb1': _L0_ffn_in['eb1'], 'L0_ffn_ew2': _L0_ffn_in['ew2'], 'L0_ffn_eb2': _L0_ffn_in['eb2'], 'L0_ffn_sw1': _L0_ffn_in['sw1'], 'L0_ffn_sb1': _L0_ffn_in['sb1'], 'L0_ffn_sw2': _L0_ffn_in['sw2'], 'L0_ffn_sb2': _L0_ffn_in['sb2']}

def reference(x, ctx_512, L0_attn_wq_down, L0_attn_wq_up, L0_attn_wq_rope, L0_attn_q_norm_w, L0_attn_wkv_down, L0_attn_kv_norm_w, L0_attn_wkv_up, L0_attn_wk_rope, L0_attn_wo, L0_xattn_Wq, L0_xattn_Wkv_expand, L0_xattn_Wout, L0_ffn_gate_w, L0_ffn_gate_b, L0_ffn_ew1, L0_ffn_eb1, L0_ffn_ew2, L0_ffn_eb2, L0_ffn_sw1, L0_ffn_sb1, L0_ffn_sw2, L0_ffn_sb2):
    import jax
    import jax.numpy as jnp

    def _L0_attn_ref(x, wq_down, wq_up, wq_rope, q_norm_w, wkv_down, kv_norm_w, wkv_up, wk_rope, wo):
        import jax, jax.numpy as jnp
        import numpy as np
        import math
        DIM = 512
        NH = 16
        Q_RANK = 384
        KV_RANK = 128
        D_NOPE = 128
        D_ROPE = 64
        D_V = 128
        EPS = 1e-06
        B, S = (2, 512)
        THETA = 10000.0

        def _rms_norm(x, w):
            return x * jax.lax.rsqrt(jnp.mean(x * x, axis=-1, keepdims=True) + EPS) * w

        def _rope_cos_sin(seq_len, d):
            inv_freq = 1.0 / THETA ** (jnp.arange(0, d, 2, dtype=jnp.float32) / d)
            t = jnp.arange(seq_len, dtype=jnp.float32)
            freqs = jnp.outer(t, inv_freq)
            return (jnp.cos(freqs), jnp.sin(freqs))

        def _apply_rope(x, cos, sin):
            x1 = x[..., 0::2]
            x2 = x[..., 1::2]
            c = cos[None, :, None, :]
            s = sin[None, :, None, :]
            o1 = x1 * c - x2 * s
            o2 = x1 * s + x2 * c
            return jnp.stack([o1, o2], axis=-1).reshape(x.shape)
        if __name__ == '__main__':
            inp = setup_inputs()
            y = jax.jit(reference)(**inp)
            print(y.shape, y.dtype)
        bs, seq_len, _ = x.shape
        q_c = _rms_norm(x @ wq_down.T, q_norm_w)
        q_nope = (q_c @ wq_up.T).reshape(bs, seq_len, NH, D_NOPE)
        q_pe = (q_c @ wq_rope.T).reshape(bs, seq_len, NH, D_ROPE)
        kv_c = _rms_norm(x @ wkv_down.T, kv_norm_w)
        kv_up = (kv_c @ wkv_up.T).reshape(bs, seq_len, NH, D_NOPE + D_V)
        k_nope = kv_up[..., :D_NOPE]
        v = kv_up[..., D_NOPE:]
        k_rope_shared = (x @ wk_rope.T).reshape(bs, seq_len, 1, D_ROPE)
        cos, sin = _rope_cos_sin(seq_len, D_ROPE)
        q_pe = _apply_rope(q_pe, cos, sin)
        k_rope_shared = _apply_rope(k_rope_shared, cos, sin)
        k_rope = jnp.broadcast_to(k_rope_shared, (bs, seq_len, NH, D_ROPE))
        q = jnp.concatenate([q_nope, q_pe], axis=-1)
        k = jnp.concatenate([k_nope, k_rope], axis=-1)
        scale = 1.0 / math.sqrt(D_NOPE + D_ROPE)
        scores = jnp.einsum('bqhd,bkhd->bhqk', q, k) * scale
        causal = jnp.tril(jnp.ones((seq_len, seq_len), dtype=bool))
        scores = jnp.where(causal[None, None], scores, -jnp.inf)
        probs = jax.nn.softmax(scores.astype(jnp.float32), axis=-1).astype(q.dtype)
        out = jnp.einsum('bhqk,bkhd->bqhd', probs, v)
        out = out.reshape(bs, seq_len, NH * D_V)
        return out @ wo.T

    def _L0_xattn_ref(q, latent_kv, Wq, Wkv_expand, Wout):
        import jax, jax.numpy as jnp
        import numpy as np
        B, S, H, NH, L = (2, 512, 512, 16, 128)
        HD = H // NH
        b, sq, _ = q.shape
        sk = latent_kv.shape[1]
        qp = q @ Wq.T
        kv = latent_kv @ Wkv_expand.T
        k, v = jnp.split(kv, 2, axis=-1)
        qh = qp.reshape(b, sq, NH, HD).transpose(0, 2, 1, 3)
        kh = k.reshape(b, sk, NH, HD).transpose(0, 2, 1, 3)
        vh = v.reshape(b, sk, NH, HD).transpose(0, 2, 1, 3)
        inv_sqrt_d = 1.0 / jnp.sqrt(jnp.float32(HD))
        scores = jnp.einsum('bhqd,bhkd->bhqk', qh, kh) * inv_sqrt_d
        causal = jnp.tril(jnp.ones((sq, sk), dtype=bool))
        scores = jnp.where(causal, scores, jnp.finfo(scores.dtype).min)
        attn = jax.nn.softmax(scores, axis=-1)
        out = jnp.einsum('bhqk,bhkd->bhqd', attn, vh)
        out = out.transpose(0, 2, 1, 3).reshape(b, sq, H)
        return out @ Wout.T

    def _L0_ffn_ref(x, gate_w, gate_b, ew1, eb1, ew2, eb2, sw1, sb1, sw2, sb2):
        import jax, jax.numpy as jnp
        import numpy as np
        D = 512
        E = 16
        TOP_K = 2
        S_EXP = 2
        H_R = D // E * 4
        H_S = D * 4
        B, S = (4, 512)
        b, s, d = x.shape
        xf = x.reshape(-1, d)
        gates = jax.nn.softmax(xf @ gate_w + gate_b, axis=-1)
        topv, topi = jax.lax.top_k(gates, TOP_K)
        combine = jnp.sum(jax.nn.one_hot(topi, E, dtype=xf.dtype) * topv[..., None], axis=1)
        h = jax.nn.gelu(jnp.einsum('nd,edh->neh', xf, ew1) + eb1, approximate=False)
        eo = jnp.einsum('neh,ehd->ned', h, ew2) + eb2
        routed = jnp.einsum('ned,ne->nd', eo, combine)
        hs = jax.nn.gelu(jnp.einsum('nd,sdh->snh', xf, sw1) + sb1[:, None, :], approximate=False)
        shared = jnp.einsum('snh,shd->nd', hs, sw2) + jnp.sum(sb2, axis=0)
        return (shared + routed).reshape(b, s, d)
    x = _layernorm(x + _L0_attn_ref(x, L0_attn_wq_down, L0_attn_wq_up, L0_attn_wq_rope, L0_attn_q_norm_w, L0_attn_wkv_down, L0_attn_kv_norm_w, L0_attn_wkv_up, L0_attn_wk_rope, L0_attn_wo), axis=-1)
    x = _layernorm(x + _L0_xattn_ref(x, ctx_512, L0_xattn_Wq, L0_xattn_Wkv_expand, L0_xattn_Wout), axis=-1)
    x = _layernorm(x + _L0_ffn_ref(x, L0_ffn_gate_w, L0_ffn_gate_b, L0_ffn_ew1, L0_ffn_eb1, L0_ffn_ew2, L0_ffn_eb2, L0_ffn_sw1, L0_ffn_sb1, L0_ffn_sw2, L0_ffn_sb2), axis=-1)
    return x

_drawn_inputs = setup_inputs


def setup_inputs(seed=0):
    import zlib

    import numpy as np

    out = dict(_drawn_inputs(seed))
    spreads = {'L0_attn_q_norm_w': (1.0, 0.6),
     'L0_attn_kv_norm_w': (1.0, 0.6),
     'L0_ffn_gate_b': (0.0, 0.8),
     'L0_ffn_eb1': (0.0, 0.8),
     'L0_ffn_eb2': (0.0, 0.496),
     'L0_ffn_sb1': (0.0, 0.1),
     'L0_ffn_sb2': (0.0, 0.1)}
    factors = {'L0_attn_wq_down': 8.0,
     'L0_attn_wq_up': 8.0,
     'L0_attn_wq_rope': 8.0,
     'L0_attn_wk_rope': 8.0,
     'L0_xattn_Wq': 8.0,
     'L0_ffn_gate_w': 3.284,
     'L0_ffn_ew1': 6.286,
     'L0_ffn_ew2': 5.905}
    for name, (base, spread) in spreads.items():
        noise = np.random.default_rng([zlib.crc32(name.encode()), seed]).standard_normal(out[name].shape)
        drawn = base * np.exp(spread * noise) if base else spread * noise
        out[name] = jnp.asarray(drawn.astype(out[name].dtype))
    for name, factor in factors.items():
        out[name] = (out[name] * factor).astype(out[name].dtype)
    return out
```

```python
from collections import namedtuple
from contextlib import ExitStack

import concourse.bass as bass
from concourse import mybir

ALU = mybir.AluOpType
ACT = mybir.ActivationFunctionType
AX = mybir.AxisListType.X
F32 = mybir.dt.float32
F32R = mybir.dt.float32r
BF16 = mybir.dt.bfloat16

P = 128
B, S, D = 8, 112, 512
CTX = 375
T = B * S
TT = T // P
HALF = T // 2
HB = B // 2
KD = D // P
NH = 16
GH = 4
NG = NH // GH
QR, LAT, DN, DR = 384, 128, 128, 64
KQ = QR // P
DXH = D // NH
E = 16
HT = 48
FG = 4
NF = HT // FG
NSH = 32 // FG
RMS_EPS, LN_EPS = 1e-6, 1e-5
ATT_SCALE = float(DN + DR) ** -0.5
X_SCALE = float(DXH) ** -0.5

A_ROPE, A_UP, A_K = 0, KQ * 256, KQ * 256 + GH * QR
A_SIZE = A_K + GH * LAT
B_V, B_O = 0, GH * LAT
B_SIZE = B_O + GH * D
A_PIECES = [(0, A_UP), (A_UP, A_UP + 1024), (A_UP + 1024, A_SIZE)]
B_PIECES = [(B_V, B_O), (B_O, B_O + 2 * D), (B_O + 2 * D, B_SIZE)]
X_Q, X_K, X_V, X_O = 0, D, D + P, D + 2 * P
X_SIZE = X_O + D
CHUNK = 2 * D
ROW = CHUNK + 2



def weave(steps, pattern, **fill):
    order = []
    for b in steps:
        for entry in pattern:
            if isinstance(entry, str):
                order += fill[entry].get(b, [])
            elif 0 <= b - entry[1] < B:
                order.append((entry[0], b - entry[1]))
    return order


def group_of(item):
    return (1, item[1:]) if item[0] == NEXT else (0, item)


NEXT = "+"
ATT_PRE = [("SA", 0), ("SA", 1), ("SA", 2), ("E", 0), ("O", 0), ("A", 0), ("A", 1), ("A", 2), ("R", 0),
           ("Q", 0, 0), ("Q", 1, 0), ("Q", 2, 0), ("Q", 3, 0), ("E", 1), ("O", 1), ("Q", 0, 1),
           ("Q", 1, 1), ("R", 1)]
_fill = {
    0: [("SB", 0), ("Q", 2, 1), ("SB", 1)],
    1: [("Q", 3, 1), ("B", 0), ("SB", 2), ("B", 1)],
    2: [("B", 2), ("B", 3)],
    3: [("W", 0), (NEXT, "SA", 0), (NEXT, "SA", 1)],
    4: [(NEXT, "E", 0), (NEXT, "O", 0), (NEXT, "SA", 2), ("W", 1)],
    5: [(NEXT, "A", 0), (NEXT, "A", 1), ("W", 2), (NEXT, "A", 2), (NEXT, "R", 0)],
    6: [("W", 3), (NEXT, "Q", 0, 0), (NEXT, "Q", 1, 0)],
    7: [(NEXT, "Q", 2, 0), (NEXT, "Q", 3, 0), ("W", 4)],
    8: [(NEXT, "E", 1), (NEXT, "O", 1)],
    9: [("W", 5), (NEXT, "Q", 0, 1), ("W", 6), (NEXT, "Q", 1, 1), (NEXT, "R", 1)]}
ATT_PE = weave(range(10), [("Z", 2), ("S", 0), ("T", 1), "fill"], fill=_fill)
ATT_ACT = weave(range(10), [("Z", 2), ("T", 1), ("S", 0), "fill"], fill=_fill)
ATT_DVE = weave(range(10), [("Z", 2), ("S", 0), ("T", 1), ("N", 0), "fill"], fill=_fill)
ATT_POOL_PRE = [("O", 0), ("R", 0), ("O", 1), ("R", 1)]
ATT_POOL = weave(range(10), [("N", 0), "c"],
                 c={4: [(NEXT, "O", 0)], 5: [(NEXT, "R", 0)], 9: [(NEXT, "O", 1), (NEXT, "R", 1)]})

X_PRE = [("L",), ("Q", 0), ("K", 0), ("V", 0)]
_fill = {
    0: [("X",)], 1: [("Q", 1)], 2: [("K", 1)], 3: [("V", 1)], 5: [(NEXT, "L"), ("W", 0)], 6: [("W", 1)],
    7: [("W", 2), (NEXT, "K", 0)], 8: [(NEXT, "Q", 0), ("W", 3)], 9: [("W", 4), (NEXT, "V", 0)],
    10: [("W", 5)], 11: [("W", 6)]}
X_PE = weave(range(12), [("S", 0), ("Z", 3), "fill", ("T", 1)], fill=_fill)
X_ACT = weave(range(12), [("Z", 3), "fill", ("S", 0), ("T", 1)], fill=_fill)
X_DVE = weave(range(12), [("S", 0), ("Z", 3), "fill", ("N", 0), ("T", 1)], fill=_fill)
X_POOL = weave(range(12), [("N", 0), "fill"], fill={0: [("X",)], 5: [(NEXT, "L")]})


class Jobs:

    def __init__(self, first, pre, body, kinds):
        self.pre = [i for i in pre if i[0] in kinds]
        self.body = [i for i in body if group_of(i)[1][0] in kinds]
        self.last = [i for i in self.body if i[0] != NEXT]
        own = self.pre + self.last
        self.per = {k: sum(i[0] == k for i in own) for k in kinds}
        self.rank = {i: sum(j[0] == i[0] for j in own[:n]) for n, i in enumerate(own)}
        self.first = first
        self.end = first + len(self.pre) + len(self.body) * (NG - 1) + len(self.last)

    def count(self, item, g):
        return self.per[item[0]] * g + self.rank[item] + 1

    def base(self, g):
        return self.first + len(self.pre) + len(self.body) * g

    def place(self, places, item, g, number):
        n = places.index(item)
        if n >= 2:
            dg, prev = group_of(places[n - 2])
        elif places is self.pre:
            return Place(n % 2, number + n, None, None)
        else:
            dg, prev = group_of([i for m, i in enumerate(self.body) if m % 2 == n][-1])
            dg -= 1
        return Place(n % 2, number + n, prev, self.count(prev, g + dg))


Place = namedtuple("Place", "bank number prev prev_count")
AJ = Jobs(0, ATT_PRE, ATT_PE, "AEOQBW")
XJ = Jobs(AJ.end, X_PRE, X_PE, "QKVW")


def turns(fori, jobs, pre, body, step, between=None):
    def run(order, places, g, number):
        for i in order:
            dg, item = group_of(i)
            step(item, g + dg, jobs.place(places, i, g, number) if i in places else None)

    run(pre, jobs.pre, 0, jobs.first)
    if between:
        between()
    with fori(0, NG - 1) as g:
        run(body, jobs.body, g, jobs.base(g))
    run([i for i in body if i[0] != NEXT], jobs.last, NG - 1, jobs.base(NG - 1))


def last_batch(tile):
    return (P * tile + P - 1) // S


def build(nc, d, scratch, out):
    with ExitStack() as ctx:
        def sb(name, shape, dt=F32, at=ctx):
            return at.enter_context(nc.sbuf_tensor(name, shape, dt))

        def pair(name, shape, at=ctx):
            return sb(name + "_hi", shape, F32R, at), sb(name + "_lo", shape, F32R, at)

        def sem(name):
            return ctx.enter_context(nc.semaphore(name))

        ps = ctx.enter_context(nc.psum_tensor("ps", [P, 8, 512], F32))

        acc = sb("acc", [P, TT, D])
        ident = sb("ident", [P, P])
        stats = sb("stats", [P, TT, 6])
        mv = sb("mv", [P, TT, 2])
        rstd = sb("rstd", [P, TT])
        stage = sb("stage", [P, A_SIZE])
        ws_hi, ws_lo = pair("ws", [P, GH * D])

        both = ctx.enter_context(ExitStack())
        identb = sb("identb", [P, S], BF16, at=both)
        maskb = sb("maskb", [P, GH * S], BF16, at=both)
        Pt = sb("Pt", [P, 2, GH * S], at=both)
        PT_hi, PT_lo = pair("PT", [P, 2, GH * S], both)
        negmax = sb("negmax", [P, 2, GH], at=both)
        rowsum = sb("rowsum", [P, 2, GH], at=both)
        rowinv = sb("rowinv", [P, 2, GH], at=both)
        cx = sb("cx", [P, B, S], at=both)

        att = ExitStack()
        qkT_hi, qkT_lo = pair("qkT", [P, KQ + 1, T], att)
        kvN_hi, kvN_lo = pair("kvN", [P, B, LAT], att)
        kr_hi, kr_lo = pair("kr", [P, T], att)
        tab = sb("tab", [P, 4, S], at=att)
        first = ExitStack()
        xT = sb("xT", [P, KD, T], at=first)
        xT_hi, xT_lo = pair("xT", [P, KD, T], first)
        wd = sb("wd", [P, KD, 768], at=first)
        wd_hi, wd_lo = pair("wd", [P, KD, 768], first)
        wnorm = sb("wnorm", [P, D], at=first)
        nat = sb("nat", [P, 4, D], at=first)
        junk = sb("junk", [P, B, D], BF16, at=first)
        ss = sb("ss", [P, B, 2], at=first)
        ss_eps = sb("ss_eps", [P, B, 2], at=first)
        ss_root = sb("ss_root", [P, B, 2], at=first)
        rinv = sb("rinv", [P, B, 2], at=first)
        krt = sb("krt", [P, 2, HALF], at=first)
        maskf = sb("maskf", [P, GH * S], at=first)
        first.close()
        wa_hi, wa_lo = pair("wa", [P, A_SIZE], att)
        qa_hi, qa_lo = pair("qa", [P, GH, T], att)
        qr = sb("qr", [P, GH, T], F32R, att)
        rt = sb("rt", [P, 2, HALF], at=att)
        ru = sb("ru", [P, 2, HALF], at=att)
        ro_hi, ro_lo = pair("ro", [P, 2, HALF], att)
        ZT_hi, ZT_lo = pair("ZT", [P, GH, T], att)
        att.close()

        xat = ExitStack()
        x1T_hi, x1T_lo = pair("x1T", [P, KD, T], xat)
        cx_hi, cx_lo = pair("cx", [P, B, S], xat)
        kb_hi, kb_lo = pair("kb", [P, B, GH, S], xat)
        vN_hi, vN_lo = pair("vN", [P, B, P], xat)
        qx_hi, qx_lo = pair("qx", [P, T], xat)
        zx_hi, zx_lo = pair("zx", [P, T], xat)
        xat.close()
        both.close()

        x2T_hi, x2T_lo = pair("x2T", [P, KD, T])
        w2_hi, w2_lo = pair("w2", [P, 2, FG, D])
        h_hi, h_lo = pair("h", [P, 2, FG, T])
        hf = sb("hf", [P, 4, HALF])
        cb = sb("cb", [P, FG, T])
        b1 = sb("b1", [P, FG])
        gw = sb("gw", [P, KD, E])
        gw_hi, gw_lo = pair("gw", [P, KD, E])
        gb = sb("gb", [P, E])
        rev = sb("rev", [P, E])
        gt = [sb(f"gt{i}", [P, TT, E]) for i in range(9)]
        g1 = sb("g1", [P, 6, TT])
        ct = sb("ct", [TT * E, P])
        e2 = sb("e2", [E + 2, D])
        e2_hi, e2_lo = pair("e2", [E + 2, D])
        cT_f = sb("cT_f", [E + 2, T])
        cT_hi, cT_lo = pair("cT", [E + 2, T])

        c_ld, acc_ld, st_ld, cx_ld, b_ld, cs_st, cT_ld, out_st = map(
            sem, "c_ld acc_ld st_ld cx_ld b_ld cs_st cT_ld out_st".split())
        x_ld = [sem(f"x_ld{k}") for k in range(KD)]
        w_ld = [sem(f"w_ld{k}") for k in range(KD)]
        pack_ld = [sem(f"pack_ld{half}") for half in range(2)]
        f_ld = [sem(f"f_ld{i}") for i in range(2)]
        cb_ld = [sem(f"cb_ld{j}") for j in range(FG)]
        (const_done, in_hi, in_lo, down_done, sq_done, eps_done, root_done, rinv_done, nat_done,
         kvn_hi, kvn_lo, tr_done, tr_hi, tr_lo, kr_done, kr_mul, kr_rot, krh, krl) = map(sem, (
            "const_done in_hi in_lo down_done sq_done eps_done root_done rinv_done nat_done kvn_hi "
            "kvn_lo tr_done tr_hi tr_lo kr_done kr_mul kr_rot krh krl").split())
        (a_hi, a_lo, bw_hi, bw_lo, xl_hi, xl_lo, xo_hi, xo_lo) = map(
            sem, "a_hi a_lo bw_hi bw_lo xl_hi xl_lo xo_hi xo_lo".split())
        a_job_hi = {k: sem(f"att_{k}_hi") for k in "AQB"}
        a_free = {k: sem(f"att_{k}_free") for k in "AEOQBW"}
        x_job_hi = {k: sem(f"x_{k}_hi") for k in "QKV"}
        x_free = {k: sem(f"x_{k}_free") for k in "QKVW"}
        (job_done, sc_done, max_done, exp_done, inv_done, norm_done, pt_done,
         pt_hi, pt_free, z_done, z_hi, z_free, rot_add, rot_hi, rot_lo) = map(sem, (
            "job_done sc_done max_done exp_done inv_done norm_done pt_done pt_hi "
            "pt_free z_done z_hi z_free rot_add rot_hi rot_lo").split())
        (ln_stat, ln_mv, ln_eps, ln_root, ln_inv, ln_out, lt_done, lt_hi, lt_lo) = map(sem, (
            "ln_stat ln_mv ln_eps ln_root ln_inv ln_out lt_done lt_hi lt_lo").split())
        kb_zero, cxs_hi, cxs_lo = map(sem, "kb_zero cxs_hi cxs_lo".split())
        (fw_hi, fw_lo, up_done, gelu_done, mix_done, h_hi_done, h_lo_done, y_done, y_free,
         cb_free) = map(sem, ("fw_hi fw_lo up_done gelu_done mix_done h_hi_done h_lo_done y_done y_free "
                              "cb_free").split())
        (g_hi, g_lo, g_done, g_step, g_exp, g_mix, g_tr, g_ct, e_one, e_hi, e_lo) = map(sem, (
            "g_hi g_lo g_done g_step g_exp g_mix g_tr g_ct e_one e_hi e_lo").split())

        def f32(ap):
            return ap.bitcast(F32)

        PASSES = 3

        def part_b(j, v_dst, o_dst):
            lo, hi = B_PIECES[j]
            return v_dst[:, A_K:A_SIZE] if j == 0 else o_dst[:, lo - B_O:hi - B_O]

        def three(w, x):
            return ((w[0], x[0]), (w[0], x[1]), (w[1], x[0]))

        ws, wa = (ws_hi, ws_lo), (wa_hi, wa_lo)
        block = ctx.enter_context(nc.Block())

        @block.sync
        def _(sp):
            for k in range(KD):
                sp.dma_start(wd[:, k, :], d["wdown"][:, k, :]).then_inc(w_ld[k], 16)
                sp.dma_start(xT[:, k, :], d["xT"][:, k, :]).then_inc(x_ld[k], 16)
            sp.dma_start(stage[:, 0:A_SIZE], d["wa"][0, :, :]).then_inc(st_ld, 16)
            for dst, name in ((ident, "ident"), (maskf, "mask"), (wnorm, "wnorm")):
                sp.dma_start(dst[:, :], d[name]).then_inc(c_ld, 16)
            sp.dma_start(tab[:, :, :], d["tab"]).then_inc(c_ld, 16)
            sp.dma_start(acc[:, :, :], d["xN"]).then_inc(acc_ld, 16)
            sp.dma_start(cx[:, :, :], d["ctxT"][:, :, 0:S]).then_inc(cx_ld, 16)

            def pack(g, half):
                sp.wait_ge(rot_lo, 2 * g + half + 2)
                for part, src in enumerate((ro_hi, ro_lo)):
                    for o in range(2):
                        for h in range(GH):
                            row = 64 * part + 32 * o
                            sp.dma_start(
                                f32(qr[row:row + 32, h, half * HALF:(half + 1) * HALF]),
                                f32(src[32 * h:32 * h + 32, o, :])).then_inc(pack_ld[half], 16)

            def load_b(g):
                sp.wait_ge(a_lo, g * len(A_PIECES) + len(A_PIECES))
                sp.dma_start(stage[:, 0:B_SIZE], d["wb"][g, :, :]).then_inc(st_ld, 16)

            load_b(0)
            pack(0, 0)
            pack(0, 1)
            with sp.Fori(1, NG) as g:
                sp.wait_ge(bw_lo, g * len(B_PIECES))
                sp.dma_start(stage[:, 0:A_SIZE], d["wa"][g, :, :]).then_inc(st_ld, 16)
                load_b(g)
                pack(g, 0)
                pack(g, 1)
            sp.wait_ge(bw_lo, NG * len(B_PIECES))
            sp.dma_start(stage[:, 0:X_SIZE], d["wx"][0, :, :]).then_inc(st_ld, 16)
            with sp.Fori(1, NG) as g:
                sp.wait_ge(xo_lo, g)
                sp.dma_start(stage[:, 0:X_SIZE], d["wx"][g, :, :]).then_inc(st_ld, 16)
            sp.wait_ge(xo_lo, NG)
            with sp.Fori(0, (4 * NF + 2) // 2) as i:
                for s in range(2):
                    sp.wait_ge(fw_lo, 2 * i + s + 1)
                    sp.dma_start(stage[:, s * ROW:(s + 1) * ROW], d["wf"][2 * i + s, :, :])\
                      .then_inc(f_ld[s], 16)
            for t in range(TT):
                sp.wait_ge(ln_out, 2 * TT + t + 1)
                sp.dma_start(out[:, t, :], acc[:, t, :]).then_inc(out_st, 16)
            sp.wait_ge(out_st, 16 * TT)

        @block.gpsimd
        def _(pool):
            def normalise(base, g, b, per):
                m = base + per * g + b
                p = Pt[0:S, b % 2, :].rearrange("p (h k) -> p h k", h=GH)
                pool.wait_ge(inv_done, m + 1)
                nc.gpsimd.tensor_tensor(p, p, rowinv[0:S, b % 2, :].unsqueeze(2).broadcast_to([S, GH, S]),
                                        ALU.mult).then_inc(norm_done, 1)

            pool.sem_inc(rot_lo, 1)

            def att_step(item, g, at):
                kind, j = item
                if kind == "O":
                    for k in "EO":
                        pool.wait_ge(a_free[k], AJ.count((k, j), g))
                    nc.gpsimd.tensor_tensor(rt[:, 0, :], rt[:, 0, :], ru[:, 0, :], ALU.subtract)
                    nc.gpsimd.tensor_tensor(rt[:, 1, :], rt[:, 1, :], ru[:, 1, :], ALU.add)\
                      .then_inc(rot_add, 1)
                elif kind == "R":
                    pool.wait_ge(rot_hi, 2 * g + j + 1)
                    pool.wait_ge(pack_ld[1 - j], 16 + 256 * (g + j))
                    if not isinstance(g, int):
                        pool.wait_ge(sc_done, B * g - B + HB * (j + 1))
                    nc.gpsimd.tensor_tensor(ro_lo[:, :, :], rt[:, :, :], f32(ro_hi[:, :, :]),
                                            ALU.subtract).then_inc(rot_lo, 1)
                elif kind == "N":
                    normalise(0, g, j, B)

            turns(pool.Fori, AJ, ATT_POOL_PRE, ATT_POOL, att_step)
            pool.wait_ge(a_free["W"], 1 + NG * TT)
            for t in (kb_hi, kb_lo):
                nc.gpsimd.memset(f32(t[:, :, :, :]), 0.0).then_inc(kb_zero, 1)

            def x_step(item, g, at):
                if item[0] == "N":
                    normalise(NG * B, g, item[1], B)
                elif item[0] == "X":
                    pool.wait_ge(xo_hi, g + 1)
                    nc.gpsimd.tensor_tensor(ws_lo[:, X_O:X_SIZE], stage[:, X_O:X_SIZE],
                                            f32(ws_hi[:, X_O:X_SIZE]), ALU.subtract).then_inc(xo_lo, 1)
                elif item[0] == "L":
                    pool.wait_ge(xl_hi, g + 1)
                    nc.gpsimd.tensor_tensor(ws_lo[:, 0:X_O], stage[:, 0:X_O], f32(ws_hi[:, 0:X_O]),
                                            ALU.subtract).then_inc(xl_lo, 1)

            turns(pool.Fori, XJ, [("L",)], X_POOL, x_step)
            pool.wait_ge(x_free["W"], 1 + NG * TT)
            for dst, name in ((gw[:, :, :], "gw"), (gb[:, :], "gb"),
                              (rev[:, :], "rev"), (e2[:, :], "e2")):
                pool.dma_start(dst, d[name]).then_inc(b_ld, 16)
            nc.gpsimd.memset(f32(cT_hi[:, :]), 1.0).then_inc(e_one, 1)
            nc.gpsimd.memset(f32(cT_lo[:, :]), 0.0).then_inc(e_one, 1)
            pool.wait_ge(g_ct, 1)
            pool.dma_start(scratch.rearrange("e (t p) -> t e p", p=P), ct[:, :]).then_inc(cs_st, 16)
            pool.wait_ge(cs_st, 16)
            pool.dma_start(cT_f[0:E, :], scratch).then_inc(cT_ld, 16)
            with pool.Fori(0, E // FG) as q:
                for j in range(FG):
                    pool.wait_ge(cb_free, FG * q + j + 1)
                    pool.dma_start(cb[:, j, :], scratch[FG * q + j, :].partition_broadcast(P))\
                        .then_inc(cb_ld[j], 16)

        @block.scalar
        def _(act):
            def copy(dst, src, **kw):
                return nc.scalar.activation(dst, src, ACT.Copy, **kw)

            for s_, n in ((exp_done, 2), (gelu_done, 4), (pack_ld[0], 16), (pack_ld[1], 16)):
                act.sem_inc(s_, n)
            for k in range(KD):
                act.wait_ge(w_ld[k], 16)
                copy(wd_hi[:, k, :], wd[:, k, :]).then_inc(in_hi, 1)
                act.wait_ge(x_ld[k], 16)
                copy(xT_hi[:, k, :], xT[:, k, :]).then_inc(in_hi, 1)
            act.wait_ge(c_ld, 64)
            copy(identb[0:S, :], ident[0:S, 0:S])
            copy(maskb[0:S, :], maskf[0:S, :]).then_inc(const_done, 1)
            for r in range(2):
                for b in range(HB * r, HB * r + HB):
                    act.wait_ge(down_done, b + 1)
                    nc.scalar.activation(junk[0:S, b, 0:QR], ps[0:S, b, 0:QR], ACT.Square,
                                         scale=float(QR) ** -0.5, accum_out=ss[0:S, b, 0:1])
                    nc.scalar.activation(junk[0:S, b, QR:QR + LAT], ps[0:S, b, QR:QR + LAT], ACT.Square,
                                         scale=float(LAT) ** -0.5, accum_out=ss[0:S, b, 1:2])\
                        .then_inc(sq_done, 1)
                act.wait_ge(eps_done, r + 1)
                nc.scalar.activation(ss_root[0:S, HB * r:HB * r + HB, :],
                                     ss_eps[0:S, HB * r:HB * r + HB, :], ACT.Sqrt).then_inc(root_done, 1)
                for b in range(HB * r, HB * r + HB):
                    act.wait_ge(nat_done, b + 1)
                    copy(kvN_hi[0:S, b, :], nat[0:S, b % 4, QR:QR + LAT]).then_inc(kvn_hi, 1)
                    act.wait_ge(tr_done, b + 1)
                    copy(qkT_hi[:, :, b * S:(b + 1) * S],
                         ps[:, b, 0:4 * S].rearrange("p (c s) -> p c s", c=4)).then_inc(tr_hi, 1)
            for half in range(2):
                act.wait_ge(kr_rot, half + 1)
                copy(kr_hi[:, half * HALF:(half + 1) * HALF], krt[:, 0, :]).then_inc(krh, 1)

            def probabilities(m, b):
                act.wait_ge(max_done, m + 1)
                for h in range(GH):
                    last = nc.scalar.activation(Pt[0:S, b % 2, h * S:(h + 1) * S],
                                                ps[0:S, b % 2, h * S:(h + 1) * S], ACT.Exp,
                                                bias=negmax[0:S, b % 2, h:h + 1],
                                                accum_out=rowsum[0:S, b % 2, h:h + 1])
                last.then_inc(exp_done, 1)

            def transposed(m, b):
                act.wait_ge(pt_done, m + 1)
                copy(PT_hi[0:S, b % 2, :], ps[0:S, 2 + b % 2, 0:GH * S]).then_inc(pt_hi, 1)

            def att_step(item, g, at):
                kind, j = item[0], item[1]
                if kind in ("A", "Q", "B"):
                    act.wait_ge(job_done, at.number + 1)
                    bank = ps[:, 6 + at.bank, :]
                    if kind == "A":
                        ins = copy(wa_hi[:, A_UP + j * D:A_UP + (j + 1) * D], bank, scale=ATT_SCALE)
                    elif kind == "B":
                        ins = copy(ws_hi[:, j * D:(j + 1) * D], bank)
                    else:
                        ins = copy(qa_hi[:, j, item[2] * HALF:(item[2] + 1) * HALF], bank[:, 0:HALF])
                    ins.then_inc(a_job_hi[kind], 1)
                elif kind == "R":
                    act.wait_ge(rot_add, 2 * g + j + 1)
                    act.wait_ge(pack_ld[1 - j], 16 + 256 * (g + j))
                    copy(ro_hi[:, :, :], rt[:, :, :]).then_inc(rot_hi, 1)
                elif kind == "SA":
                    lo, hi = A_PIECES[j]
                    act.wait_ge(st_ld, 32 * g + 16)
                    copy(wa_hi[:, lo:hi], stage[:, lo:hi]).then_inc(a_hi, 1)
                elif kind == "SB":
                    if j == 0:
                        act.wait_ge(st_ld, 32 * g + 32)
                        act.wait_ge(job_done, AJ.base(g))
                    copy(part_b(j, wa_hi, ws_hi), stage[:, slice(*B_PIECES[j])]).then_inc(bw_hi, 1)
                elif kind == "S":
                    probabilities(B * g + j, j)
                elif kind == "T":
                    transposed(B * g + j, j)
                elif kind == "Z":
                    act.wait_ge(z_done, B * g + j + 1)
                    copy(ZT_hi[:, :, j * S:(j + 1) * S],
                         ps[:, 4 + j % 2, 0:GH * S].rearrange("p (h s) -> p h s", h=GH))\
                        .then_inc(z_hi, 1)

            turns(act.Fori, AJ, ATT_PRE, ATT_ACT, att_step)

            def layernorm_root(i):
                act.wait_ge(ln_eps, i + 1)
                nc.scalar.activation(rstd[:, :], rstd[:, :], ACT.Sqrt).then_inc(ln_root, 1)

            def layernorm_turned(i, dst):
                for t in range(TT):
                    act.wait_ge(lt_done, TT * i + t + 1)
                    copy(dst[:, :, t * P:(t + 1) * P],
                         ps[:, t, :].rearrange("p (c s) -> p c s", c=KD)).then_inc(lt_hi, 1)

            layernorm_root(0)
            layernorm_turned(0, x1T_hi)
            act.wait_ge(cx_ld, 16)
            copy(cx_hi[:, :, :], cx[:, :, :]).then_inc(cxs_hi, 1)
            act.wait_ge(kb_zero, 2)

            def x_step(item, g, at):
                kind, j = item[0], item[-1]
                m = NG * B + B * g
                if kind == "L":
                    act.wait_ge(st_ld, 32 * NG + 16 * g + 16)
                    copy(ws_hi[:, 0:X_O], stage[:, 0:X_O]).then_inc(xl_hi, 1)
                elif kind == "X":
                    act.wait_ge(job_done, XJ.base(g))
                    copy(ws_hi[:, X_O:X_SIZE], stage[:, X_O:X_SIZE]).then_inc(xo_hi, 1)
                elif kind in ("Q", "K", "V"):
                    act.wait_ge(job_done, at.number + 1)
                    bank = ps[:, 6 + at.bank, :]
                    if kind == "Q":
                        ins = copy(qx_hi[:, j * HALF:(j + 1) * HALF], bank[:, 0:HALF], scale=X_SCALE)
                    elif kind == "V":
                        ins = copy(vN_hi[0:S, HB * j:HB * j + HB, :],
                                   bank[0:S, :].rearrange("p (b v) -> p b v", b=HB))
                    else:
                        for h in range(GH):
                            r = slice(DXH * h, DXH * (h + 1))
                            ins = copy(kb_hi[r, HB * j:HB * j + HB, h, :],
                                       bank[r, 0:HALF].rearrange("p (b s) -> p b s", b=HB))
                    ins.then_inc(x_job_hi[kind], 1)
                elif kind == "S":
                    probabilities(m + j, j)
                elif kind == "T":
                    transposed(m + j, j)
                elif kind == "Z":
                    act.wait_ge(z_done, m + j + 1)
                    for h in range(GH):
                        r = slice(DXH * h, DXH * (h + 1))
                        ins = copy(zx_hi[r, j * S:(j + 1) * S], ps[r, 4 + j % 2, h * S:(h + 1) * S])
                    ins.then_inc(z_hi, 1)

            turns(act.Fori, XJ, X_PRE, X_ACT, x_step)
            layernorm_root(1)

            def up_tile(n, par, j, routed):
                for half in range(2):
                    q = 2 * FG * n + 2 * j + half
                    slot = (2 * j + half) % 4
                    cols = slice(half * HALF, (half + 1) * HALF)
                    act.wait_ge(up_done, q + 1)
                    act.wait_ge(h_lo_done, q + 1)
                    bias = b1[:, j:j + 1]
                    src = ps[:, slot, 0:HALF]
                    if routed is None:
                        nc.scalar.activation(hf[:, slot, :], src, ACT.Gelu, bias=bias)
                        nc.scalar.activation(h_hi[:, par, j, cols], src, ACT.Gelu, bias=bias)\
                            .then_inc(gelu_done, 1)
                    else:
                        nc.scalar.activation(hf[:, slot, :], src, ACT.Gelu, bias=bias)\
                            .then_inc(gelu_done, 1)
                        act.wait_ge(mix_done, 2 * FG * routed + 2 * j + half + 1)
                        copy(h_hi[:, par, j, cols], hf[:, slot, :]).then_inc(h_hi_done, 1)

            act.wait_ge(job_done, XJ.end)
            for s in range(2):
                act.wait_ge(f_ld[s], 16)
                copy(ws_hi[:, s * CHUNK:(s + 1) * CHUNK], stage[:, s * ROW:s * ROW + CHUNK]).then_inc(fw_hi, 1)
            act.wait_ge(b_ld, 64)
            copy(gw_hi[:, :, :], gw[:, :, :]).then_inc(g_hi, 1)
            layernorm_turned(1, x2T_hi)
            act.wait_ge(g_step, 3)
            nc.scalar.activation(gt[1][:, :, :], gt[1][:, :, :], ACT.Exp).then_inc(g_exp, 1)

            def stage_of(n, par, routed):
                for j in range(FG):
                    up_tile(n, par, j, routed)
                    s = j % 2
                    act.wait_ge(f_ld[s], 32 * n + 16 * (2 + j // 2))
                    if s == 0:
                        dst = w2_hi[:, par, j:j + 2, :].rearrange("p j n -> p (j n)")
                    else:
                        dst = ws_hi[:, (j - 1) * D:(j + 1) * D]
                    copy(dst, stage[:, s * ROW:s * ROW + CHUNK]).then_inc(fw_hi, 1)

            stage_of(0, 0, None)
            act.wait_ge(cT_ld, 16)
            act.wait_ge(e_one, 2)
            copy(cT_hi[0:E, :], cT_f[0:E, :]).then_inc(e_hi, 1)
            copy(e2_hi[:, :], e2[:, :]).then_inc(e_hi, 1)
            with act.Fori(0, (NSH - 2) // 2) as i:
                stage_of(2 * i + 1, 1, None)
                stage_of(2 * i + 2, 0, None)
            stage_of(NSH - 1, 1, None)
            with act.Fori(0, (NF - NSH) // 2) as i:
                stage_of(2 * i + NSH, 0, 2 * i)
                stage_of(2 * i + NSH + 1, 1, 2 * i + 1)
            for t in range(TT):
                act.wait_ge(ln_eps, 2 + t + 1)
                nc.scalar.activation(rstd[:, t:t + 1], rstd[:, t:t + 1], ACT.Sqrt).then_inc(ln_root, 1)

        @block.vector
        def _(dve):
            def low(dst, src, hi, **kw):
                return nc.vector.tensor_tensor(dst, src, f32(hi), ALU.subtract)

            def low_scaled(dst, src, hi, scale):
                return nc.vector.scalar_tensor_tensor(dst, src, scale, f32(hi), ALU.mult, ALU.subtract)

            for s_, n in ((pt_free, 2), (z_free, 2), (fw_lo, 2), (h_lo_done, 4),
                          (y_free, 4), (cb_free, FG), (a_free["W"], 1), (x_free["W"], 1)):
                dve.sem_inc(s_, n)
            for k in range(KD):
                dve.wait_ge(in_hi, 2 * k + 1)
                low(wd_lo[:, k, :], wd[:, k, :], wd_hi[:, k, :]).then_inc(in_lo, 1)
                dve.wait_ge(in_hi, 2 * k + 2)
                low(xT_lo[:, k, :], xT[:, k, :], xT_hi[:, k, :]).then_inc(in_lo, 1)
            dve.wait_ge(c_ld, 64)
            for r in range(2):
                rows = slice(HB * r, HB * r + HB)
                dve.wait_ge(sq_done, HB * r + HB)
                nc.vector.tensor_scalar(ss_eps[0:S, rows, :], ss[0:S, rows, :], RMS_EPS, None, ALU.add)\
                  .then_inc(eps_done, 1)
                dve.wait_ge(root_done, r + 1)
                nc.vector.reciprocal(rinv[0:S, rows, :], ss_root[0:S, rows, :]).then_inc(rinv_done, 1)
                dve.wait_ge(rinv_done, r + 1)
                for b in range(HB * r, HB * r + HB):
                    if b >= 4:
                        dve.wait_ge(tr_done, b - 3)
                        dve.wait_ge(kvn_hi, b - 3)
                    for q, (lo, hi) in enumerate(((0, QR), (QR, QR + LAT))):
                        ins = nc.vector.scalar_tensor_tensor(nat[0:S, b % 4, lo:hi], ps[0:S, b, lo:hi],
                                                             rinv[0:S, b, q:q + 1], wnorm[0:S, lo:hi],
                                                             ALU.mult, ALU.mult)
                    ins.then_inc(nat_done, 1)
                for b in range(HB * r, HB * r + HB):
                    dve.wait_ge(kvn_hi, b + 1)
                    low(kvN_lo[0:S, b, :], nat[0:S, b % 4, QR:QR + LAT], kvN_hi[0:S, b, :])\
                        .then_inc(kvn_lo, 1)
                    dve.wait_ge(tr_hi, b + 1)
                    cols = slice(b * S, (b + 1) * S)
                    low(qkT_lo[:, :, cols], ps[:, b, 0:4 * S].rearrange("p (c s) -> p c s", c=4),
                        qkT_hi[:, :, cols]).then_inc(tr_lo, 1)

            def table(i):
                return tab[:, i, :].unsqueeze(1).broadcast_to([P, HB, S])

            def batches(ap):
                return ap.rearrange("p (b s) -> p b s", b=HB)

            for half in range(2):
                if half:
                    dve.wait_ge(krl, half)
                for s in range(2):
                    dve.wait_ge(kr_done, 2 * half + s + 1)
                    ins = nc.vector.tensor_tensor(batches(krt[:, s, :]),
                                                  batches(ps[:, 2 * half + s, 0:HALF]), table(2 + s),
                                                  ALU.mult)
                ins.then_inc(kr_mul, 1)
                dve.wait_ge(kr_mul, half + 1)
                nc.vector.tensor_tensor(krt[:, 0, :], krt[:, 0, :], krt[:, 1, :], ALU.add)\
                  .then_inc(kr_rot, 1)
                dve.wait_ge(krh, half + 1)
                cols = slice(half * HALF, (half + 1) * HALF)
                low(kr_lo[:, cols], krt[:, 0, :], kr_hi[:, cols]).then_inc(krl, 1)
            dve.wait_ge(acc_ld, 16)

            def row_max(m, b):
                dve.wait_ge(sc_done, m + 1)
                nc.vector.tensor_reduce(negmax[0:S, b % 2, :],
                                        ps[0:S, b % 2, 0:GH * S].rearrange("p (h k) -> p h k", h=GH),
                                        AX, ALU.max, negate=True).then_inc(max_done, 1)

            def row_inverse(m, b):
                dve.wait_ge(exp_done, m + 3)
                nc.vector.reciprocal(rowinv[0:S, b % 2, :], rowsum[0:S, b % 2, :]).then_inc(inv_done, 1)

            def transposed(m, b):
                dve.wait_ge(pt_hi, m + 1)
                low(PT_lo[0:S, b % 2, :], ps[0:S, 2 + b % 2, 0:GH * S], PT_hi[0:S, b % 2, :])\
                    .then_inc(pt_free, 1)

            def add_output(at, t, free):
                dve.wait_ge(job_done, at.number + 1)
                nc.vector.tensor_tensor(acc[:, t, :], ps[:, 6 + at.bank, :], acc[:, t, :], ALU.add)\
                  .then_inc(free, 1)

            def att_step(item, g, at):
                kind, j = item[0], item[1]
                m = B * g + j
                if kind in ("A", "Q", "B"):
                    dve.wait_ge(a_job_hi[kind], AJ.count(item, g))
                    bank = ps[:, 6 + at.bank, :]
                    if kind == "A":
                        cols = slice(A_UP + j * D, A_UP + (j + 1) * D)
                        ins = low_scaled(wa_lo[:, cols], bank, wa_hi[:, cols], ATT_SCALE)
                    elif kind == "B":
                        cols = slice(j * D, (j + 1) * D)
                        ins = low(ws_lo[:, cols], bank, ws_hi[:, cols])
                    else:
                        cols = slice(item[2] * HALF, (item[2] + 1) * HALF)
                        ins = low(qa_lo[:, j, cols], bank[:, 0:HALF], qa_hi[:, j, cols])
                    ins.then_inc(a_free[kind], 1)
                elif kind in "EO":
                    dst = rt if kind == "E" else ru
                    tabs = (0, 1) if kind == "E" else (1, 0)
                    dve.wait_ge(job_done, at.number + 1)
                    if kind == "E":
                        dve.wait_ge(rot_lo, 2 * g + j + 1)
                    for i in range(2):
                        ins = nc.vector.tensor_tensor(batches(dst[:, i, :]),
                                                      batches(ps[:, 6 + at.bank, 0:HALF]),
                                                      table(tabs[i]), ALU.mult)
                    ins.then_inc(a_free[kind], 1)
                elif kind == "SA":
                    lo, hi = A_PIECES[j]
                    dve.wait_ge(a_hi, len(A_PIECES) * g + j + 1)
                    low(wa_lo[:, lo:hi], stage[:, lo:hi], wa_hi[:, lo:hi]).then_inc(a_lo, 1)
                elif kind == "SB":
                    dve.wait_ge(bw_hi, len(B_PIECES) * g + j + 1)
                    low(part_b(j, wa_lo, ws_lo), stage[:, slice(*B_PIECES[j])],
                        part_b(j, wa_hi, ws_hi)).then_inc(bw_lo, 1)
                elif kind == "S":
                    row_max(m, j)
                elif kind == "N":
                    row_inverse(m, j)
                elif kind == "T":
                    transposed(m, j)
                elif kind == "Z":
                    dve.wait_ge(z_hi, m + 1)
                    cols = slice(j * S, (j + 1) * S)
                    low(ZT_lo[:, :, cols], ps[:, 4 + j % 2, 0:GH * S].rearrange("p (h s) -> p h s", h=GH),
                        ZT_hi[:, :, cols]).then_inc(z_free, 1)
                elif kind == "W":
                    add_output(at, j, a_free["W"])

            turns(dve.Fori, AJ, ATT_PRE, ATT_DVE, att_step)

            def layernorm_stats(i):
                for t in range(TT):
                    ins = nc.vector.bn_stats(stats[:, t, :], acc[:, t, :])
                ins.then_inc(ln_stat, 1)
                dve.wait_ge(ln_stat, i + 1)
                for t in range(TT):
                    ins = nc.vector.bn_aggr(mv[:, t, :], stats[:, t, :])
                ins.then_inc(ln_mv, 1)
                dve.wait_ge(ln_mv, i + 1)
                nc.vector.tensor_scalar(rstd[:, :], mv[:, :, 1], LN_EPS, None, ALU.add).then_inc(ln_eps, 1)
                dve.wait_ge(ln_root, i + 1)
                nc.vector.reciprocal(rstd[:, :], rstd[:, :]).then_inc(ln_inv, 1)
                dve.wait_ge(ln_inv, i + 1)
                for t in range(TT):
                    nc.vector.tensor_scalar(acc[:, t, :], acc[:, t, :], mv[:, t, 0:1], rstd[:, t:t + 1],
                                            ALU.subtract, ALU.mult).then_inc(ln_out, 1)

            def layernorm_turned(i, dst, hi):
                for t in range(TT):
                    dve.wait_ge(lt_hi, TT * i + t + 1)
                    cols = slice(t * P, (t + 1) * P)
                    low(dst[:, :, cols], ps[:, t, :].rearrange("p (c s) -> p c s", c=KD), hi[:, :, cols])\
                        .then_inc(lt_lo, 1)

            dve.wait_ge(a_free["W"], 1 + NG * TT)
            layernorm_stats(0)
            layernorm_turned(0, x1T_lo, x1T_hi)
            dve.wait_ge(cxs_hi, 1)
            low(cx_lo[:, :, :], cx[:, :, :], cx_hi[:, :, :]).then_inc(cxs_lo, 1)

            def x_step(item, g, at):
                kind, j = item[0], item[-1]
                m = NG * B + B * g
                if kind in ("Q", "K", "V"):
                    dve.wait_ge(x_job_hi[kind], XJ.count(item, g))
                    bank = ps[:, 6 + at.bank, :]
                    bs = slice(HB * j, HB * j + HB)
                    if kind == "Q":
                        cols = slice(j * HALF, (j + 1) * HALF)
                        ins = low_scaled(qx_lo[:, cols], bank[:, 0:HALF], qx_hi[:, cols], X_SCALE)
                    elif kind == "V":
                        ins = low(vN_lo[0:S, bs, :], bank[0:S, :].rearrange("p (b v) -> p b v", b=HB),
                                  vN_hi[0:S, bs, :])
                    else:
                        for h in range(GH):
                            r = slice(DXH * h, DXH * (h + 1))
                            ins = low(kb_lo[r, bs, h, :],
                                      bank[r, 0:HALF].rearrange("p (b s) -> p b s", b=HB),
                                      kb_hi[r, bs, h, :])
                    ins.then_inc(x_free[kind], 1)
                elif kind == "S":
                    row_max(m + j, j)
                elif kind == "N":
                    row_inverse(m + j, j)
                elif kind == "T":
                    transposed(m + j, j)
                elif kind == "Z":
                    dve.wait_ge(z_hi, m + j + 1)
                    cols = slice(j * S, (j + 1) * S)
                    for h in range(GH):
                        r = slice(DXH * h, DXH * (h + 1))
                        ins = low(zx_lo[r, cols], ps[r, 4 + j % 2, h * S:(h + 1) * S], zx_hi[r, cols])
                    ins.then_inc(z_free, 1)
                elif kind == "W":
                    add_output(at, j, x_free["W"])

            turns(dve.Fori, XJ, X_PRE, X_DVE, x_step)
            dve.wait_ge(x_free["W"], 1 + NG * TT)
            layernorm_stats(1)
            for i in range(2):
                dve.wait_ge(fw_hi, i + 1)
                cols = slice(i * CHUNK, (i + 1) * CHUNK)
                nc.vector.tensor_copy(b1[:, 2 * i:2 * i + 2], stage[:, i * ROW + CHUNK:(i + 1) * ROW])
                low(ws_lo[:, cols], stage[:, i * ROW:i * ROW + CHUNK], ws_hi[:, cols]).then_inc(fw_lo, 1)
            dve.wait_ge(g_hi, 1)
            low(gw_lo[:, :, :], gw[:, :, :], gw_hi[:, :, :]).then_inc(g_lo, 1)
            layernorm_turned(1, x2T_lo, x2T_hi)

            step = [0]

            def then(ins):
                step[0] += 1
                ins.then_inc(g_step, 1)
                dve.wait_ge(g_step, step[0])

            def wide(ap):
                return ap.unsqueeze(2).broadcast_to([P, TT, E])

            def per_expert(ap):
                return ap[:, :].unsqueeze(1).broadcast_to([P, TT, E])

            def gates():
                V = nc.vector
                dve.wait_ge(g_done, 1)
                logits, soft, eq1, sel1, rest, eq2, sel2, both_, mix = gt
                then(V.tensor_tensor(logits[:, :, :], ps[:, 7, 0:TT * E].rearrange("p (t e) -> p t e", t=TT),
                                     per_expert(gb), ALU.add))
                then(V.tensor_reduce(g1[:, 0, :], logits[:, :, :], AX, ALU.max))
                then(V.tensor_tensor(soft[:, :, :], logits[:, :, :], wide(g1[:, 0, :]), ALU.subtract))
                dve.wait_ge(g_exp, 1)
                then(V.tensor_reduce(g1[:, 1, :], soft[:, :, :], AX, ALU.add))
                then(V.reciprocal(g1[:, 2, :], g1[:, 1, :]))
                then(V.tensor_tensor(soft[:, :, :], soft[:, :, :], wide(g1[:, 2, :]), ALU.mult))
                left = soft
                for k, (eq, sel) in enumerate(((eq1, sel1), (eq2, sel2))):
                    then(V.tensor_reduce(g1[:, 3, :], left[:, :, :], AX, ALU.max))
                    then(V.tensor_tensor(eq[:, :, :], left[:, :, :], wide(g1[:, 3, :]), ALU.is_equal))
                    then(V.tensor_tensor(eq[:, :, :], eq[:, :, :], per_expert(rev), ALU.mult))
                    then(V.tensor_reduce(g1[:, 4, :], eq[:, :, :], AX, ALU.max))
                    then(V.tensor_tensor(sel[:, :, :], eq[:, :, :], wide(g1[:, 4, :]), ALU.is_equal))
                    if k == 0:
                        then(V.scalar_tensor_tensor(rest[:, :, :], sel[:, :, :], -4.0, soft[:, :, :],
                                                    ALU.mult, ALU.add))
                        left = rest
                then(V.tensor_tensor(both_[:, :, :], sel1[:, :, :], sel2[:, :, :], ALU.add))
                V.tensor_tensor(mix[:, :, :], both_[:, :, :], soft[:, :, :], ALU.mult).then_inc(g_mix, 1)
                dve.wait_ge(g_tr, 1)
                V.tensor_copy(ct[:, :], ps[0:TT * E, 7, 0:P]).then_inc(g_ct, 1)

            def up_tile(n, par, j, routed):
                for half in range(2):
                    q = 2 * FG * n + 2 * j + half
                    slot = (2 * j + half) % 4
                    cols = slice(half * HALF, (half + 1) * HALF)
                    dve.wait_ge(gelu_done, q + 5)
                    if routed is not None:
                        if half == 0:
                            dve.wait_ge(cb_ld[j], 16 * routed + 16)
                        ins = nc.vector.tensor_tensor(hf[:, slot, :], hf[:, slot, :], cb[:, j, cols],
                                                      ALU.mult)
                        ins.then_inc(mix_done, 1)
                        dve.wait_ge(h_hi_done, 2 * FG * routed + 2 * j + half + 1)
                        if half == 1:
                            dve.sem_inc(cb_free, 1)
                    low(h_lo[:, par, j, cols], hf[:, slot, :], h_hi[:, par, j, cols])\
                        .then_inc(h_lo_done, 1)

            def down_tile(n, t):
                dve.wait_ge(y_done, TT * n + t + 1)
                nc.vector.tensor_tensor(acc[:, t, :], ps[:, 4 + t % 4, :], acc[:, t, :], ALU.add)\
                  .then_inc(y_free, 1)

            def stage_of(n, par, routed, down=True):
                tiles = [(0, 1), (2, 3), (4, 5), (6,)]
                for j in range(FG):
                    up_tile(n, par, j, routed)
                    if down:
                        for t in tiles[j]:
                            down_tile(n - 1, t)
                    s = j % 2
                    dve.wait_ge(fw_hi, 4 * n + 3 + j)
                    if s == 0:
                        dst, hi = (x[:, par, j:j + 2, :].rearrange("p j n -> p (j n)") for x in (w2_lo, w2_hi))
                    else:
                        dst, hi = (x[:, (j - 1) * D:(j + 1) * D] for x in (ws_lo, ws_hi))
                        nc.vector.tensor_copy(b1[:, j - 1:j + 1], stage[:, s * ROW + CHUNK:(s + 1) * ROW])
                    low(dst, stage[:, s * ROW:s * ROW + CHUNK], hi).then_inc(fw_lo, 1)

            gates()
            stage_of(0, 0, None, down=False)
            dve.wait_ge(e_hi, 1)
            low(cT_lo[0:E, :], cT_f[0:E, :], cT_hi[0:E, :]).then_inc(e_lo, 1)
            dve.wait_ge(e_hi, 2)
            low(e2_lo[:, :], e2[:, :], e2_hi[:, :]).then_inc(e_lo, 1)
            with dve.Fori(0, (NSH - 2) // 2) as i:
                stage_of(2 * i + 1, 1, None)
                stage_of(2 * i + 2, 0, None)
            stage_of(NSH - 1, 1, None)
            with dve.Fori(0, (NF - NSH) // 2) as i:
                stage_of(2 * i + NSH, 0, 2 * i)
                stage_of(2 * i + NSH + 1, 1, 2 * i + 1)
            for t in range(TT):
                down_tile(NF - 1, t)
                dve.wait_ge(y_free, 4 + TT * (NF - 1) + t + 1)
                nc.vector.bn_stats(stats[:, t, :], acc[:, t, :]).then_inc(ln_stat, 1)
                dve.wait_ge(ln_stat, 2 + t + 1)
                nc.vector.bn_aggr(mv[:, t, :], stats[:, t, :]).then_inc(ln_mv, 1)
                dve.wait_ge(ln_mv, 2 + t + 1)
                nc.vector.tensor_scalar(rstd[:, t:t + 1], mv[:, t, 1:2], LN_EPS, None, ALU.add)\
                  .then_inc(ln_eps, 1)
                dve.wait_ge(ln_root, 2 + t + 1)
                nc.vector.reciprocal(rstd[:, t:t + 1], rstd[:, t:t + 1]).then_inc(ln_inv, 1)
                dve.wait_ge(ln_inv, 2 + t + 1)
                nc.vector.tensor_scalar(acc[:, t, :], acc[:, t, :], mv[:, t, 0:1], rstd[:, t:t + 1],
                                        ALU.subtract, ALU.mult).then_inc(ln_out, 1)

        @block.tensor
        def _(pe):
            mm = nc.tensor.matmul

            def product(dst, terms, start=True, stop=True):
                ops = [p for w, x in terms for p in three(w, x)]
                for i, (w, x) in enumerate(ops):
                    ins = mm(dst, w, x, start=start and i == 0, stop=stop and i == len(ops) - 1,
                             skip_group_check=not (start and stop))
                return ins

            def two(hl, *idx):
                return tuple(x[idx] for x in hl)

            for r in range(2):
                for k in range(KD):
                    if r == 0:
                        pe.wait_ge(in_lo, 2 * k + 2)
                    for b in range(HB * r, HB * r + HB):
                        ops = three(two((xT_hi, xT_lo), slice(None), k, slice(b * S, (b + 1) * S)),
                                    two((wd_hi, wd_lo), slice(None), k, slice(0, D)))
                        for i, (w, x) in enumerate(ops):
                            ins = mm(ps[0:S, b, :], w, x, start=k == 0 and i == 0,
                                     stop=k == KD - 1 and i == 2)
                        if k == KD - 1:
                            ins.then_inc(down_done, 1)
            for b in range(B):
                pe.wait_ge(nat_done, b + 1)
                for c in range(4):
                    ins = nc.tensor.transpose(ps[:, b, c * S:(c + 1) * S], nat[0:S, b % 4, c * P:(c + 1) * P],
                                              ident[0:S, 0:S])
                ins.then_inc(tr_done, 1)
            for half in range(2):
                for s in range(2):
                    bank = 2 * half + s
                    pe.wait_ge(tr_lo, bank + 1)
                    cols = slice(half * HALF, (half + 1) * HALF)
                    product(ps[:, bank, 0:HALF],
                            [(two((wd_hi, wd_lo), slice(None), k, slice(D + P * s, D + P * s + P)),
                              two((xT_hi, xT_lo), slice(None), k, cols)) for k in range(KD)])\
                        .then_inc(kr_done, 1)
            pe.wait_ge(tr_lo, B)
            pe.wait_ge(kvn_lo, B)
            pe.wait_ge(krl, 2)
            pe.wait_ge(const_done, 1)

            def mask(b):
                mm(ps[0:S, b % 2, 0:GH * S], identb[0:S, :], maskb[0:S, :], start=True, stop=False,
                   skip_group_check=True)

            def transposes(m, b):
                pe.wait_ge(norm_done, m + 1)
                pe.wait_ge(pt_free, m + 1)
                for h in range(GH):
                    ins = nc.tensor.transpose(ps[0:S, 2 + b % 2, h * S:(h + 1) * S],
                                              Pt[0:S, b % 2, h * S:(h + 1) * S], ident[0:S, 0:S])
                ins.then_inc(pt_done, 1)

            def weigh(m, b, w):
                pe.wait_ge(pt_free, m + 3)
                pe.wait_ge(z_free, m + 1)
                product(ps[:, 4 + b % 2, 0:GH * S],
                        [(w, two((PT_hi, PT_lo), slice(0, S), b % 2, slice(None)))]).then_inc(z_done, 1)

            def bank_free(free, at):
                if at and at.prev:
                    pe.wait_ge(free[at.prev[0]], at.prev_count + (at.prev[0] == "W"))

            def att_step(item, g, at):
                kind, j = item[0], item[1]
                if at:
                    bank_free(a_free, at)
                    bank = ps[:, 6 + at.bank, :]
                if kind in "EO":
                    pe.wait_ge(a_lo, len(A_PIECES) * g + 1)
                    off = A_ROPE + (0 if kind == "E" else P)
                    cols = slice(j * HALF, (j + 1) * HALF)
                    ins = product(bank[:, 0:HALF],
                                  [(two(wa, slice(None), slice(off + 256 * c, off + 256 * c + P)),
                                    two((qkT_hi, qkT_lo), slice(None), c, cols)) for c in range(KQ)])
                elif kind == "A":
                    pe.wait_ge(a_lo, len(A_PIECES) * (g + 1))
                    for h in range(GH):
                        u, k = A_UP + j * D + h * P, A_K + h * LAT
                        ins = product(bank[:, h * LAT:(h + 1) * LAT],
                                      [(two(wa, slice(None), slice(u, u + P)),
                                        two(wa, slice(None), slice(k, k + LAT)))])
                elif kind == "Q":
                    pe.wait_ge(a_free["A"], AJ.count(("A", KQ - 1), g))
                    cols = slice(item[2] * HALF, (item[2] + 1) * HALF)
                    ins = product(bank[:, 0:HALF],
                                  [(two(wa, slice(None), slice(A_UP + c * D + j * LAT,
                                                               A_UP + c * D + (j + 1) * LAT)),
                                    two((qkT_hi, qkT_lo), slice(None), c, cols)) for c in range(KQ)])
                elif kind == "B":
                    pe.wait_ge(bw_lo, len(B_PIECES) * g + (2 if j < 2 else 3))
                    v = A_K + j * LAT
                    ins = product(bank, [(two(wa, slice(None), slice(v, v + LAT)),
                                          two(ws, slice(None), slice(j * D, (j + 1) * D)))])
                elif kind == "W":
                    pe.wait_ge(z_free, 2 + B * g + last_batch(j) + 1)
                    pe.wait_ge(a_free["B"], AJ.count(("B", GH - 1), g))
                    ins = product(bank, [(two((ZT_hi, ZT_lo), slice(None), h, slice(j * P, (j + 1) * P)),
                                          two(ws, slice(None), slice(h * D, (h + 1) * D)))
                                         for h in range(GH)])
                if at:
                    ins.then_inc(job_done, 1)
                if kind == "S":
                    pe.wait_ge(exp_done, B * g + j + 1)
                    pe.wait_ge(a_free["Q"], AJ.count(("Q", GH - 1, j // HB), g))
                    pe.wait_ge(pack_ld[j // HB], 16 + 256 * (g + 1))
                    mask(j)
                    tok = slice(j * S, (j + 1) * S)
                    for h in range(GH):
                        dst = ps[0:S, j % 2, h * S:(h + 1) * S]
                        product(dst, [(two((qa_hi, qa_lo), slice(None), h, tok),
                                       two((qkT_hi, qkT_lo), slice(None), KQ, tok))],
                                start=False, stop=False)
                        for i, k in enumerate((kr_hi, kr_lo)):
                            ins = mm(dst, qr[:, h, tok], k[:, tok], start=False,
                                     stop=h == GH - 1 and i == 1, skip_group_check=True)
                    ins.then_inc(sc_done, 1)
                elif kind == "T":
                    transposes(B * g + j, j)
                elif kind == "Z":
                    weigh(B * g + j, j, two((kvN_hi, kvN_lo), slice(0, S), j, slice(None)))

            turns(pe.Fori, AJ, ATT_PRE, ATT_PE, att_step,
                  lambda: pe.wait_ge(a_free["Q"], AJ.count(AJ.pre[-1], 0)))

            def turn(i):
                for t in range(TT):
                    pe.wait_ge(ln_out, TT * i + t + 1)
                    for c in range(KD):
                        ins = nc.tensor.transpose(ps[:, t, c * P:(c + 1) * P], acc[:, t, c * P:(c + 1) * P],
                                                  ident[:, :])
                    ins.then_inc(lt_done, 1)

            turn(0)
            pe.wait_ge(lt_lo, TT)
            pe.wait_ge(cxs_lo, 1)

            def x_step(item, g, at):
                kind, j = item[0], item[-1]
                m = NG * B + B * g
                if at:
                    bank_free(x_free, at)
                    bank = ps[:, 6 + at.bank, :]
                if kind in ("Q", "K", "V"):
                    pe.wait_ge(xl_lo, g + 1)
                    cols = slice(j * HALF, (j + 1) * HALF)
                    ctx_half = tuple(x[:, HB * j:HB * j + HB, :].rearrange("p b s -> p (b s)")
                                     for x in (cx_hi, cx_lo))
                if kind == "Q":
                    ins = product(bank[:, 0:HALF],
                                  [(two(ws, slice(None), slice(X_Q + P * k, X_Q + P * k + P)),
                                    two((x1T_hi, x1T_lo), slice(None), k, cols)) for k in range(KD)])
                elif kind == "K":
                    ins = product(bank[:, 0:HALF], [(two(ws, slice(None), slice(X_K, X_K + P)), ctx_half)])
                elif kind == "V":
                    for b in range(HB):
                        ins = product(bank[0:S, b * P:(b + 1) * P],
                                      [(two((cx_hi, cx_lo), slice(None), HB * j + b, slice(None)),
                                        two(ws, slice(None), slice(X_V, X_V + P)))])
                elif kind == "W":
                    pe.wait_ge(z_free, 2 + m + last_batch(j) + 1)
                    pe.wait_ge(xo_lo, g + 1)
                    ins = product(bank, [(two((zx_hi, zx_lo), slice(None), slice(j * P, (j + 1) * P)),
                                          two(ws, slice(None), slice(X_O, X_O + D)))])
                if at:
                    ins.then_inc(job_done, 1)
                if kind == "S":
                    pe.wait_ge(exp_done, m + j + 1)
                    pe.wait_ge(x_free["K"], XJ.count(("K", j // HB), g))
                    pe.wait_ge(x_free["Q"], XJ.count(("Q", j // HB), g))
                    mask(j)
                    keys = tuple(x[:, j, :, :].rearrange("p h s -> p (h s)") for x in (kb_hi, kb_lo))
                    ops = three(two((qx_hi, qx_lo), slice(None), slice(j * S, (j + 1) * S)), keys)
                    for i, (w, x) in enumerate(ops):
                        ins = mm(ps[0:S, j % 2, 0:GH * S], w, x, start=False, stop=i == 2,
                                 skip_group_check=True)
                    ins.then_inc(sc_done, 1)
                elif kind == "T":
                    transposes(m + j, j)
                elif kind == "Z":
                    pe.wait_ge(x_free["V"], XJ.count(("V", j // HB), g))
                    weigh(m + j, j, two((vN_hi, vN_lo), slice(0, S), j, slice(None)))

            turns(pe.Fori, XJ, X_PRE, X_PE, x_step,
                  lambda: pe.wait_ge(x_free["V"], XJ.count(XJ.pre[-1], 0)))
            turn(1)
            pe.wait_ge(lt_lo, 2 * TT)
            pe.wait_ge(g_lo, 1)
            for t in range(TT):
                for k in range(KD):
                    w = two((x2T_hi, x2T_lo), slice(None), k, slice(t * P, (t + 1) * P))
                    x = two((gw_hi, gw_lo), slice(None), k, slice(None))
                    ops = [(a, b_) for a in w for b_ in x]
                    for i, (a, b_) in enumerate(ops):
                        ins = mm(ps[:, 7, t * E:(t + 1) * E], a, b_, start=k == 0 and i == 0,
                                 stop=k == KD - 1 and i == len(ops) - 1)
            ins.then_inc(g_done, 1)

            def up_tile(n, j):
                chunk = j // 2 if isinstance(n, int) and n == 0 else 4 * n - 1 + 2 * (j // 2)
                pe.wait_ge(fw_lo, 2 + chunk + 1)
                for half in range(2):
                    q = 2 * FG * n + 2 * j + half
                    pe.wait_ge(gelu_done, q + 1)
                    product(ps[:, (2 * j + half) % 4, 0:HALF],
                            [(two(ws, slice(None), slice(D * j + P * k, D * j + P * k + P)),
                              two((x2T_hi, x2T_lo), slice(None), k, slice(half * HALF, (half + 1) * HALF)))
                             for k in range(KD)]).then_inc(up_done, 1)

            def down_tile(n, par, t, biases=False):
                if t == 0:
                    pe.wait_ge(h_lo_done, 4 + 2 * FG * n + 2 * FG)
                    pe.wait_ge(fw_lo, 2 + 4 * n + 5)
                pe.wait_ge(y_free, TT * n + t + (2 if t < 3 else 1))
                tok = slice(t * P, (t + 1) * P)
                dst = ps[:, 4 + t % 4, :]
                if biases:
                    product(dst, [(two((cT_hi, cT_lo), slice(None), tok), two((e2_hi, e2_lo), slice(None), slice(None)))],
                            stop=False)
                product(dst, [(two((h_hi, h_lo), slice(None), par, j, tok),
                               two((w2_hi, w2_lo), slice(None), par, j, slice(None))) for j in range(FG)],
                        start=not biases).then_inc(y_done, 1)

            def stage_of(n, par, down=True):
                tiles = [(0, 1), (2, 3), (4, 5), (6,)]
                for j in range(FG):
                    up_tile(n, j)
                    if down:
                        for t in tiles[j]:
                            down_tile(n - 1, 1 - par, t)

            stage_of(0, 0, down=False)
            pe.wait_ge(g_mix, 1)
            nc.tensor.transpose(ps[0:TT * E, 7, 0:P], gt[8][:, :, :].rearrange("p t e -> p (t e)"), ident[:, :])\
              .then_inc(g_tr, 1)
            pe.wait_ge(g_ct, 1)
            with pe.Fori(0, (NSH - 2) // 2) as i:
                stage_of(2 * i + 1, 1)
                stage_of(2 * i + 2, 0)
            stage_of(NSH - 1, 1)
            with pe.Fori(0, (NF - NSH) // 2) as i:
                stage_of(2 * i + NSH, 0)
                stage_of(2 * i + NSH + 1, 1)
            pe.wait_ge(e_lo, 2)
            for t in range(TT):
                down_tile(NF - 1, 1, t, biases=True)


def layouts(inputs):
    import numpy as np

    def a(name):
        return np.asarray(inputs[name])

    o = {}
    x = a("x").reshape(T, D)
    o["xT"] = x.T.reshape(KD, P, T).transpose(1, 0, 2)
    o["xN"] = x.reshape(TT, P, D).transpose(1, 0, 2)
    o["ctxT"] = a("ctx_512").transpose(2, 0, 1)
    kr = a("L0_attn_wk_rope")
    x1, x2 = kr[0::2], kr[1::2]
    down = np.concatenate([a("L0_attn_wq_down"), a("L0_attn_wkv_down"), x1, x2, x1, x2, x2, x1, x2, x1])
    o["wdown"] = down.T.reshape(KD, P, 768).transpose(1, 0, 2)
    o["wnorm"] = np.broadcast_to(np.concatenate([a("L0_attn_q_norm_w"), a("L0_attn_kv_norm_w")]), (P, D))
    rope = a("L0_attn_wq_rope").reshape(NG, GH, DR // 2, 2, KQ, P).transpose(0, 5, 4, 3, 1, 2)
    up = a("L0_attn_wq_up").reshape(NG, GH, DN, KQ, P).transpose(0, 2, 3, 1, 4)
    kv = a("L0_attn_wkv_up").reshape(NG, GH, 2, DN, LAT).transpose(2, 0, 3, 1, 4)
    wo = a("L0_attn_wo").reshape(D, NG, GH, DN).transpose(1, 3, 2, 0)
    flat = lambda z: z.reshape(NG, P, -1)
    o["wa"] = np.concatenate([flat(rope), flat(up), flat(kv[0])], axis=2)
    o["wb"] = np.concatenate([flat(kv[1]), flat(wo)], axis=2)
    wq = a("L0_xattn_Wq").reshape(NG, P, KD, P).transpose(0, 3, 2, 1)
    wk, wv = a("L0_xattn_Wkv_expand").reshape(2, NG, P, P).transpose(0, 1, 3, 2)
    wout = a("L0_xattn_Wout").reshape(D, NG, P).transpose(1, 2, 0)
    o["wx"] = np.concatenate([flat(wq), flat(wk), flat(wv), flat(wout)], axis=2)
    w1s = a("L0_ffn_sw1").reshape(2, KD, P, 16, P).transpose(0, 3, 2, 1, 4).reshape(32, P, D)
    w1e = a("L0_ffn_ew1").reshape(E, KD, P, P).transpose(0, 2, 1, 3).reshape(E, P, D)
    w1 = np.concatenate([w1s, w1e])
    w2 = np.concatenate([a("L0_ffn_sw2").reshape(32, P, D), a("L0_ffn_ew2")])
    pairs = lambda w: w.reshape(HT // 2, 2, P, D).transpose(0, 2, 1, 3).reshape(HT // 2, P, CHUNK)
    b1 = np.concatenate([a("L0_ffn_sb1").reshape(32, P), a("L0_ffn_eb1")])
    none = np.zeros((HT // 2, P, 2), np.float32)
    w1 = np.concatenate([pairs(w1), b1.reshape(HT // 2, 2, P).transpose(0, 2, 1)], axis=2)
    w2 = np.concatenate([pairs(w2), none], axis=2)
    order = [w1[0], w1[1]]
    for n in range(NF):
        last = n == NF - 1
        order += [w2[2 * n], np.zeros_like(w1[0]) if last else w1[2 * n + 2],
                  w2[2 * n + 1], np.zeros_like(w1[0]) if last else w1[2 * n + 3]]
    o["wf"] = np.stack(order)
    o["gw"] = a("L0_ffn_gate_w").reshape(KD, P, E).transpose(1, 0, 2)
    o["gb"] = np.broadcast_to(a("L0_ffn_gate_b"), (P, E))
    o["e2"] = np.concatenate([a("L0_ffn_eb2"), a("L0_ffn_sb2")])
    f = np.float32
    inv = (f(1.0) / f(10000.0) ** (np.arange(0, DR, 2, dtype=f) / f(DR))).astype(f)
    ang = np.outer(np.arange(S, dtype=f), inv).astype(f)
    c, s = np.tile(np.cos(ang).T, (4, 1)), np.tile(np.sin(ang).T, (4, 1))
    sign = np.repeat(np.array([-1, 1, -1, 1], f), 32)[:, None]
    o["tab"] = np.stack([c * f(ATT_SCALE), s * f(ATT_SCALE), c, s * sign], axis=1)
    o["ident"] = np.eye(P, dtype=f)
    m = np.zeros((P, GH, S), f)
    m[np.arange(P)[:, None, None] < np.arange(S)[None, None, :] + np.zeros((1, GH, 1), int)] = -3.0e38
    o["mask"] = m.reshape(P, GH * S)
    o["rev"] = np.broadcast_to((E - np.arange(E)).astype(f), (P, E))
    return {k: np.ascontiguousarray(v) for k, v in o.items()}


def kernel(**inputs):
    import concourse.bacc as bacc
    from concourse.bass_utils import run_bass_kernel_spmd

    nc = bacc.Bacc("TRN2", target_bir_lowering=False, num_devices=1)
    arrays = layouts(inputs)
    d = {k: nc.dram_tensor(f"in_{k}", v.shape, F32, kind="ExternalInput").ap() for k, v in arrays.items()}
    scratch = nc.dram_tensor("mix_scratch", (E, T), F32, kind="Internal").ap()
    out = nc.dram_tensor("out", (T, D), F32, kind="ExternalOutput").ap()
    build(nc, d, scratch, out.rearrange("(t p) n -> p t n", p=P))
    r = run_bass_kernel_spmd(nc, [{f"in_{k}": v for k, v in arrays.items()}], core_ids=[0])
    return r.results[0]["out"].reshape(B, S, D)
```

```python
from collections import namedtuple
from contextlib import ExitStack

import concourse.bass as bass
from concourse import mybir

ALU = mybir.AluOpType
ACT = mybir.ActivationFunctionType
AX = mybir.AxisListType.X
F32 = mybir.dt.float32
F32R = mybir.dt.float32r
BF16 = mybir.dt.bfloat16

P = 128
B, S, D = 8, 112, 512
CTX = 375
T = B * S
TT = T // P
HALF = T // 2
HB = B // 2
KD = D // P
NH = 16
GH = 4
NG = NH // GH
QR, LAT, DN, DR = 384, 128, 128, 64
KQ = QR // P
DXH = D // NH
E = 16
HT = 48
FG = 4
NF = HT // FG
NSH = 32 // FG
RMS_EPS, LN_EPS = 1e-6, 1e-5
ATT_SCALE = float(DN + DR) ** -0.5
X_SCALE = float(DXH) ** -0.5

A_ROPE, A_UP, A_K = 0, KQ * 256, KQ * 256 + GH * QR
A_SIZE = A_K + GH * LAT
B_V, B_O = 0, GH * LAT
B_SIZE = B_O + GH * D
A_PIECES = [(0, A_UP), (A_UP, A_UP + 1024), (A_UP + 1024, A_SIZE)]
B_PIECES = [(B_V, B_O), (B_O, B_O + 2 * D), (B_O + 2 * D, B_SIZE)]
X_Q, X_K, X_V, X_O = 0, D, D + P, D + 2 * P
X_SIZE = X_O + D
CHUNK = 2 * D
ROW = CHUNK + 2



NEXT, LAST = "+", "!"


def weave(steps, pattern, wrap=False, **fill):
    order = []
    for b in steps:
        for entry in pattern:
            if isinstance(entry, str):
                order += fill[entry].get(b, [])
            elif 0 <= b - entry[1] < B:
                order.append((entry[0], b - entry[1]))
            elif wrap and b - entry[1] >= B:
                order.append((NEXT, entry[0], b - entry[1] - B))
    return order


def group_of(item):
    return (1, item[1:]) if item[0] == NEXT else (0, item)


LN_PARTS = [(0, TT - 2), (TT - 2, TT)]
ATT_PRE = [("E", 0), ("O", 0), ("A", 0), ("R", 0), ("E", 1), ("A", 1), ("A", 2), ("O", 1), ("Q", 0, 0),
           ("R", 1), ("Q", 1, 0), ("Q", 2, 0), ("Q", 3, 0), ("Q", 0, 1), ("G", 0), ("SB", 0), ("Q", 1, 1)]
_fill = {
    0: [("SB", 1), ("G", 1), ("Q", 2, 1), ("SB", 2), ("G", 2), ("B", 0), ("B", 1)],
    1: [("B", 2), ("Q", 3, 1)],
    2: [("G", 3), (NEXT, "SA", 0), ("G", 4)],
    3: [("G", 5), ("B", 3), (NEXT, "SA", 1), (NEXT, "SA", 2), (NEXT, "E", 0), (NEXT, "O", 0)],
    4: [("W", 0), (NEXT, "A", 0), ("G", 6), (NEXT, "R", 0)],
    5: [("W", 1), (NEXT, "E", 1), ("G", 7)],
    6: [(NEXT, "A", 1), ("W", 2), (NEXT, "A", 2), (NEXT, "O", 1)],
    7: [(NEXT, "Q", 0, 0), ("W", 3), (NEXT, "R", 1)],
    8: [(LAST, "CX"), (LAST, "L"), (NEXT, "Q", 1, 0), ("W", 4), (LAST, "LN1", 0), (NEXT, "Q", 2, 0),
        (NEXT, "Q", 3, 0), (NEXT, "Q", 0, 1)],
    9: [(LAST, "U1", 0), (LAST, "U1", 1), (LAST, "U1", 2), (NEXT, "G", 0), ("W", 5), (LAST, "U1", 3),
        (LAST, "U1", 4), (NEXT, "SB", 0), (NEXT, "Q", 1, 1), ("W", 6), (LAST, "LN1", 1)]}
ATT_PE = weave(range(10), [("Z", 2), ("S", 0), ("T", 1), "fill"], fill=_fill)
ATT_ACT = weave(range(10), [("Z", 2), ("T", 1), ("S", 0), "fill"], fill=_fill)
ATT_DVE = weave(range(10), [("S", 0), ("T", 1), ("Z", 2), ("N", 0), "fill"], fill=_fill)
ATT_POOL_PRE = [("O", 0), ("R", 0), ("O", 1), ("R", 1)]
ATT_POOL = weave(range(10), [("N", 0), "fill"],
                 fill={3: [(NEXT, "O", 0)], 4: [(NEXT, "R", 0)], 6: [(NEXT, "O", 1)], 7: [(NEXT, "R", 1)],
                       8: [(LAST, "CX"), (LAST, "L"), (LAST, "KB")]})

X_START = [("V", 0), ("K", 0), ("Q", 0), ("U1", 5), ("U1", 6)]
_first = {2: [("K", 1), ("Q", 1)], 3: [("V", 1)]}
_fill = {
    4: [(NEXT, "L")],
    5: [("X",)],
    6: [(NEXT, "K", 0), (NEXT, "Q", 0)],
    7: [(NEXT, "V", 0), ("W", 0), (LAST, "G", 0)],
    8: [("W", 1), ("W", 2), (LAST, "F", 0)],
    9: [("W", 3), ("W", 4), (LAST, "LN2", 0)],
    10: [(LAST, "U2", 0), (LAST, "U2", 1), (LAST, "U2", 2), (NEXT, "K", 1), (NEXT, "Q", 1)],
    11: [("W", 5), (LAST, "U2", 3), (LAST, "U2", 4), (NEXT, "V", 1), ("W", 6), (LAST, "LN2", 1), (LAST, "F", 1)]}
_pe = [("Z", 3), ("S", 0), "fill", ("T", 1)]
_act = [("Z", 3), "fill", ("S", 0), ("T", 1)]
_dve = [("S", 0), ("Z", 3), "fill", ("N", 0), ("T", 1)]
X_PRE_PE, X_PRE_ACT, X_PRE_DVE = (X_START + weave(range(4), p, fill=_first) for p in (_pe, _act, _dve))
X_PE, X_ACT, X_DVE = (weave(range(4, 12), p, wrap=True, fill=_fill) for p in (_pe, _act, _dve))
X_PRE_POOL = weave(range(4), [("N", 0)])
X_POOL = weave(range(4, 12), [("N", 0), "fill"], wrap=True, fill={4: [(NEXT, "L")], 5: [("X",)]})


class Jobs:

    def __init__(self, first, pre, body, kinds):
        self.pre = [i for i in pre if i[0] in kinds]
        self.body = [i for i in body if group_of(i)[1][0] in kinds]
        self.last = [i for i in self.body if i[0] != NEXT]
        own = self.pre + self.last
        self.per = {k: sum(i[0] == k for i in own) for k in kinds}
        self.rank = {i: sum(j[0] == i[0] for j in own[:n]) for n, i in enumerate(own)}
        self.first = first
        self.end = first + len(self.pre) + len(self.body) * (NG - 1) + len(self.last)

    def count(self, item, g):
        return self.per[item[0]] * g + self.rank[item] + 1

    def base(self, g):
        return self.first + len(self.pre) + len(self.body) * g

    def place(self, places, item, g, number):
        n = places.index(item)
        if n >= 2:
            dg, prev = group_of(places[n - 2])
        elif places is self.pre:
            return Place(n % 2, number + n, None, None)
        else:
            dg, prev = group_of([i for m, i in enumerate(self.body) if m % 2 == n][-1])
            dg -= 1
        return Place(n % 2, number + n, prev, self.count(prev, g + dg))


Place = namedtuple("Place", "bank number prev prev_count")
AJ = Jobs(0, ATT_PRE, ATT_PE, "AEOQGBW")
XJ = Jobs(AJ.end, X_PRE_PE, X_PE, "QKVW")


def turns(fori, jobs, pre, body, step, between=None):
    def run(order, places, g, number):
        for i in order:
            dg, item = group_of(i[1:] if i[0] == LAST else i)
            step(item, g + dg, jobs.place(places, i, g, number) if i in places else None)

    run(pre, jobs.pre, 0, jobs.first)
    if between:
        between()
    with fori(0, NG - 1) as g:
        run([i for i in body if i[0] != LAST], jobs.body, g, jobs.base(g))
    run([i for i in body if i[0] != NEXT], jobs.last, NG - 1, jobs.base(NG - 1))


def last_batch(tile):
    return (P * tile + P - 1) // S


def build(nc, d, scratch, out):
    with ExitStack() as ctx:
        def sb(name, shape, dt=F32, at=ctx):
            return at.enter_context(nc.sbuf_tensor(name, shape, dt))

        def pair(name, shape, at=ctx):
            return sb(name + "_hi", shape, F32R, at), sb(name + "_lo", shape, F32R, at)

        def sem(name):
            return ctx.enter_context(nc.semaphore(name))

        ps = ctx.enter_context(nc.psum_tensor("ps", [P, 8, 512], F32))

        acc = sb("acc", [P, TT, D])
        ident = sb("ident", [P, P])
        stats = sb("stats", [P, TT, 6])
        mv = sb("mv", [P, TT, 2])
        rstd = sb("rstd", [P, TT])
        stage = sb("stage", [P, A_SIZE])
        ws_hi, ws_lo = pair("ws", [P, GH * D])

        both = ctx.enter_context(ExitStack())
        identb = sb("identb", [P, S], BF16, at=both)
        maskb = sb("maskb", [P, S], BF16, at=both)
        Pt = sb("Pt", [P, 2, GH * S], at=both)
        PT_hi, PT_lo = pair("PT", [P, 2, GH * S], both)
        negmax = sb("negmax", [P, 2, GH], at=both)
        rowsum = sb("rowsum", [P, 2, GH], at=both)
        rowinv = sb("rowinv", [P, 2, GH], at=both)

        att = ExitStack()
        first = ExitStack()
        xT = sb("xT", [P, KD, T], at=first)
        wd = sb("wd", [P, KD, 768], at=first)
        xT_hi, xT_lo = pair("xT", [P, KD, T], first)
        wd_hi, wd_lo = pair("wd", [P, KD, 768], first)
        wnorm = sb("wnorm", [P, D], at=first)
        nat = sb("nat", [P, 4, D], at=first)
        junk = sb("junk", [P, B, D], BF16, at=first)
        ss = sb("ss", [P, B, 2], at=first)
        ss_eps = sb("ss_eps", [P, B, 2], at=first)
        ss_root = sb("ss_root", [P, B, 2], at=first)
        rinv = sb("rinv", [P, B, 2], at=first)
        krt = sb("krt", [P, 2, HALF], at=first)
        maskf = sb("maskf", [P, S], at=first)
        first.close()
        wa_hi, wa_lo = pair("wa", [P, A_SIZE], att)
        rt = sb("rt", [P, 2, HALF], at=att)
        ru = sb("ru", [P, 2, HALF], at=att)
        ro_hi, ro_lo = pair("ro", [P, 2, HALF], att)
        qa_hi, qa_lo = pair("qa", [P, GH, T], att)
        qr = sb("qr", [P, GH, T], F32R, att)
        ZT_hi, ZT_lo = pair("ZT", [P, GH, T], att)
        qkT_hi, qkT_lo = pair("qkT", [P, KQ + 1, T], att)
        kvN_hi, kvN_lo = pair("kvN", [P, B, LAT], att)
        kr_hi, kr_lo = pair("kr", [P, T], att)
        tab = sb("tab", [P, 4, S], at=att)
        sT = sb("sT", [P, 2, GH * S], at=att)
        att.close()

        xat = ExitStack()
        x1T_hi, x1T_lo = pair("x1T", [P, KD, T], xat)
        kb_hi, kb_lo = pair("kb", [P, B, GH, S], xat)
        cx = sb("cx", [P, B, S], at=xat)
        cx_hi, cx_lo = pair("cx", [P, B, S], xat)
        wx_hi, wx_lo = pair("wx", [P, X_SIZE], xat)
        vN_hi, vN_lo = pair("vN", [P, B, P], xat)
        qx_hi, qx_lo = pair("qx", [P, T], xat)
        zx_hi, zx_lo = pair("zx", [P, T], xat)
        xat.close()
        both.close()

        w2_hi, w2_lo = pair("w2", [P, 2, FG, D])
        h_hi, h_lo = pair("h", [P, 2, FG, T])
        hf = sb("hf", [P, 4, HALF])
        cb = sb("cb", [P, FG, T])
        gt = [sb(f"gt{i}", [P, TT, E]) for i in range(9)]
        g1 = sb("g1", [P, 6, TT])
        x2T_hi, x2T_lo = pair("x2T", [P, KD, T])
        b1 = sb("b1", [P, FG])
        gw = sb("gw", [P, KD, E])
        gw_hi, gw_lo = pair("gw", [P, KD, E])
        gb = sb("gb", [P, E])
        rev = sb("rev", [P, E])
        lg = sb("lg", [E, T])
        ct = sb("ct", [TT * E, P])
        e2 = sb("e2", [E + 2, D])
        e2_hi, e2_lo = pair("e2", [E + 2, D])
        cT_f = sb("cT_f", [E + 2, T])
        cT_hi, cT_lo = pair("cT", [E + 2, T])

        xo_ld, x2_ld, wk_ld, c_ld, acc_ld, st_ld, cx_ld, b_ld, cs_st, cT_ld, out_st = map(
            sem, "xo_ld x2_ld wk_ld c_ld acc_ld st_ld cx_ld b_ld cs_st cT_ld out_st".split())
        x_ld = [sem(f"x_ld{k}") for k in range(KD)]
        w_ld = [sem(f"w_ld{k}") for k in range(KD)]
        pack_ld = [sem(f"pack_ld{half}") for half in range(2)]
        f_ld = [sem(f"f_ld{i}") for i in range(2)]
        cb_ld = [sem(f"cb_ld{j}") for j in range(FG)]
        (const_done, in_hi, in_lo, down_done, sq_done, eps_done, root_done, rinv_done, nat_done,
         kvn_hi, kvn_lo, tr_done, tr_hi, tr_lo, kr_done, kr_mul, kr_rot, krh, krl) = map(sem, (
            "const_done in_hi in_lo down_done sq_done eps_done root_done rinv_done nat_done kvn_hi "
            "kvn_lo tr_done tr_hi tr_lo kr_done kr_mul kr_rot krh krl").split())
        (a_hi, a_lo, bw_hi, bw_lo, xl_hi, xl_lo, xo_hi, xo_lo) = map(
            sem, "a_hi a_lo bw_hi bw_lo xl_hi xl_lo xo_hi xo_lo".split())
        a_job_hi = {k: sem(f"att_{k}_hi") for k in "AQB"}
        a_free = {k: sem(f"att_{k}_free") for k in "AEOQGBW"}
        x_job_hi = {k: sem(f"x_{k}_hi") for k in "QKV"}
        x_free = {k: sem(f"x_{k}_free") for k in "QKVW"}
        (job_done, sc_done, max_done, exp_done, inv_done, norm_done, pt_done,
         pt_hi, pt_free, z_done, z_hi, z_free, rot_add, rot_hi, rot_lo) = map(sem, (
            "job_done sc_done max_done exp_done inv_done norm_done pt_done pt_hi "
            "pt_free z_done z_hi z_free rot_add rot_hi rot_lo").split())
        (ln_stat, ln_mv, ln_eps, ln_root, ln_inv, ln_out, lt_done, lt_hi, lt_lo) = map(sem, (
            "ln_stat ln_mv ln_eps ln_root ln_inv ln_out lt_done lt_hi lt_lo").split())
        kb_zero, cxs_hi, cxs_lo = map(sem, "kb_zero cxs_hi cxs_lo".split())
        (fw_hi, fw_lo, up_done, gelu_done, mix_done, h_hi_done, h_lo_done, y_done, y_free,
         cb_free) = map(sem, ("fw_hi fw_lo up_done gelu_done mix_done h_hi_done h_lo_done y_done y_free "
                              "cb_free").split())
        (g_hi, g_lo, g_log, g_lg, g_done, g_step, g_exp, g_mix, g_tr, g_ct, e_one, e_hi, e_lo) = map(sem, (
            "g_hi g_lo g_log g_lg g_done g_step g_exp g_mix g_tr g_ct e_one e_hi e_lo").split())

        def f32(ap):
            return ap.bitcast(F32)

        PASSES = 3

        def part_b(j, v_dst, o_dst):
            lo, hi = B_PIECES[j]
            return v_dst[:, A_K:A_SIZE] if j == 0 else o_dst[:, lo - B_O:hi - B_O]

        def three(w, x):
            return ((w[0], x[0]), (w[0], x[1]), (w[1], x[0]))

        ws, wa, wx = (ws_hi, ws_lo), (wa_hi, wa_lo), (wx_hi, wx_lo)
        block = ctx.enter_context(nc.Block())

        @block.sync
        def _(sp):
            for k in range(KD):
                sp.dma_start(wd[:, k, 0:D], d["wdown"][:, k, 0:D]).then_inc(w_ld[k], 16)
                sp.dma_start(xT[:, k, 0:HALF], d["xT"][:, k, 0:HALF]).then_inc(x_ld[k], 16)
            sp.dma_start(xT[:, :, HALF:T], d["xT"][:, :, HALF:T]).then_inc(x2_ld, 16)
            sp.dma_start(wd[:, :, D:768], d["wdown"][:, :, D:768]).then_inc(wk_ld, 16)
            for dst, name in ((ident, "ident"), (maskf, "mask"), (wnorm, "wnorm")):
                sp.dma_start(dst[:, :], d[name]).then_inc(c_ld, 16)
            sp.dma_start(tab[:, :, :], d["tab"]).then_inc(c_ld, 16)
            sp.dma_start(stage[:, 0:A_SIZE], d["wa"][0, :, :]).then_inc(st_ld, 16)
            sp.dma_start(acc[:, :, :], d["xN"]).then_inc(acc_ld, 16)

            def pack(g, half):
                sp.wait_ge(rot_lo, 2 * g + half + 2)
                for part, src in enumerate((ro_hi, ro_lo)):
                    for o in range(2):
                        for h in range(GH):
                            row = 64 * part + 32 * o
                            sp.dma_start(
                                f32(qr[row:row + 32, h, half * HALF:(half + 1) * HALF]),
                                f32(src[32 * h:32 * h + 32, o, :])).then_inc(pack_ld[half], 16)

            def load_b(g):
                sp.wait_ge(a_lo, g * len(A_PIECES) + len(A_PIECES))
                sp.dma_start(stage[:, 0:B_SIZE], d["wb"][g, :, :]).then_inc(st_ld, 16)

            load_b(0)
            pack(0, 0)
            pack(0, 1)
            with sp.Fori(1, NG) as g:
                sp.wait_ge(bw_lo, g * len(B_PIECES))
                sp.dma_start(stage[:, 0:A_SIZE], d["wa"][g, :, :]).then_inc(st_ld, 16)
                load_b(g)
                pack(g, 0)
                pack(g, 1)
            sp.wait_ge(bw_lo, NG * len(B_PIECES))
            sp.dma_start(stage[:, 0:X_O], d["wx"][0, :, 0:X_O]).then_inc(st_ld, 16)
            sp.dma_start(stage[:, X_O:X_SIZE], d["wx"][0, :, X_O:X_SIZE]).then_inc(xo_ld, 16)
            sp.wait_ge(sc_done, B * NG)
            sp.dma_start(cx[:, :, :], d["ctxT"][:, :, 0:S]).then_inc(cx_ld, 16)
            with sp.Fori(1, NG) as g:
                sp.wait_ge(xl_lo, g)
                sp.dma_start(stage[:, 0:X_O], d["wx"][g, :, 0:X_O]).then_inc(st_ld, 16)
                sp.wait_ge(xo_lo, g)
                sp.dma_start(stage[:, X_O:X_SIZE], d["wx"][g, :, X_O:X_SIZE]).then_inc(xo_ld, 16)
            sp.wait_ge(xo_lo, NG)
            with sp.Fori(0, (4 * NF + 2) // 2) as i:
                for s in range(2):
                    sp.wait_ge(fw_lo, 2 * i + s + 1)
                    sp.dma_start(stage[:, s * ROW:(s + 1) * ROW], d["wf"][2 * i + s, :, :])\
                      .then_inc(f_ld[s], 16)
            for t in range(TT):
                sp.wait_ge(ln_out, 2 * TT + t + 1)
                sp.dma_start(out[:, t, :], acc[:, t, :]).then_inc(out_st, 16)
            sp.wait_ge(out_st, 16 * TT)

        @block.gpsimd
        def _(pool):
            def normalise(base, g, b, per):
                m = base + per * g + b
                p = Pt[0:S, b % 2, :].rearrange("p (h k) -> p h k", h=GH)
                pool.wait_ge(inv_done, m + 1)
                nc.gpsimd.tensor_tensor(p, p, rowinv[0:S, b % 2, :].unsqueeze(2).broadcast_to([S, GH, S]),
                                        ALU.mult).then_inc(norm_done, 1)

            def low_l(g):
                pool.wait_ge(xl_hi, g + 1)
                nc.gpsimd.tensor_tensor(wx_lo[:, 0:X_O], stage[:, 0:X_O], f32(wx_hi[:, 0:X_O]),
                                        ALU.subtract).then_inc(xl_lo, 1)

            pool.sem_inc(rot_lo, 1)
            for i, (lo, hi) in enumerate(A_PIECES):
                pool.wait_ge(a_hi, i + 1)
                nc.gpsimd.tensor_tensor(wa_lo[:, lo:hi], stage[:, lo:hi], f32(wa_hi[:, lo:hi]),
                                        ALU.subtract).then_inc(a_lo, 1)

            def att_step(item, g, at):
                kind, j = item[0], item[-1]
                if kind == "O":
                    for k in "EO":
                        pool.wait_ge(a_free[k], AJ.count((k, j), g))
                    nc.gpsimd.tensor_tensor(rt[:, 0, :], rt[:, 0, :], ru[:, 0, :], ALU.subtract)
                    nc.gpsimd.tensor_tensor(rt[:, 1, :], rt[:, 1, :], ru[:, 1, :], ALU.add)\
                      .then_inc(rot_add, 1)
                elif kind == "R":
                    pool.wait_ge(rot_hi, 2 * g + j + 1)
                    pool.wait_ge(pack_ld[1 - j], 16 + 256 * (g + j))
                    if not isinstance(g, int):
                        pool.wait_ge(sc_done, B * g - B + HB * (j + 1))
                    nc.gpsimd.tensor_tensor(ro_lo[:, :, :], rt[:, :, :], f32(ro_hi[:, :, :]),
                                            ALU.subtract).then_inc(rot_lo, 1)
                elif kind == "N":
                    normalise(0, g, j, B)
                elif kind == "CX":
                    pool.wait_ge(cxs_hi, 1)
                    nc.gpsimd.tensor_tensor(cx_lo[:, :, :], cx[:, :, :], f32(cx_hi[:, :, :]), ALU.subtract)\
                      .then_inc(cxs_lo, 1)
                elif kind == "KB":
                    pool.wait_ge(sc_done, B * NG)
                    for t in (kb_hi, kb_lo):
                        nc.gpsimd.memset(f32(t[:, :, :, :]), 0.0).then_inc(kb_zero, 1)
                elif kind == "L":
                    low_l(0)

            turns(pool.Fori, AJ, ATT_POOL_PRE, ATT_POOL, att_step)
            pool.wait_ge(a_free["W"], 1 + NG * TT)
            for dst, name in ((gw[:, :, :], "gw"), (gb[:, :], "gb"),
                              (rev[:, :], "rev"), (e2[:, :], "e2")):
                pool.dma_start(dst, d[name]).then_inc(b_ld, 16)
            nc.gpsimd.memset(f32(cT_hi[:, :]), 1.0).then_inc(e_one, 1)
            nc.gpsimd.memset(f32(cT_lo[:, :]), 0.0).then_inc(e_one, 1)

            def x_step(item, g, at):
                if item[0] == "N":
                    normalise(NG * B, g, item[1], B)
                elif item[0] == "X":
                    pool.wait_ge(xo_hi, g + 1)
                    nc.gpsimd.tensor_tensor(wx_lo[:, X_O:X_SIZE], stage[:, X_O:X_SIZE],
                                            f32(wx_hi[:, X_O:X_SIZE]), ALU.subtract).then_inc(xo_lo, 1)
                elif item[0] == "L":
                    low_l(g)

            turns(pool.Fori, XJ, X_PRE_POOL, X_POOL, x_step)
            pool.wait_ge(g_ct, 1)
            pool.dma_start(scratch.rearrange("e (t p) -> t e p", p=P), ct[:, :]).then_inc(cs_st, 16)
            pool.wait_ge(cs_st, 16)
            pool.dma_start(cT_f[0:E, :], scratch).then_inc(cT_ld, 16)
            with pool.Fori(0, E // FG) as q:
                for j in range(FG):
                    pool.wait_ge(cb_free, FG * q + j + 1)
                    pool.dma_start(cb[:, j, :], scratch[FG * q + j, :].partition_broadcast(P))\
                        .then_inc(cb_ld[j], 16)

        @block.scalar
        def _(act):
            def copy(dst, src, **kw):
                return nc.scalar.activation(dst, src, ACT.Copy, **kw)

            for s_, n in ((exp_done, 2), (gelu_done, 4), (pack_ld[0], 16), (pack_ld[1], 16)):
                act.sem_inc(s_, n)
            for k in range(KD):
                act.wait_ge(w_ld[k], 16)
                copy(wd_hi[:, k, 0:D], wd[:, k, 0:D]).then_inc(in_hi, 1)
                act.wait_ge(x_ld[k], 16)
                copy(xT_hi[:, k, 0:HALF], xT[:, k, 0:HALF]).then_inc(in_hi, 1)
            act.wait_ge(x2_ld, 16)
            copy(xT_hi[:, :, HALF:T], xT[:, :, HALF:T]).then_inc(in_hi, 1)
            act.wait_ge(wk_ld, 16)
            copy(wd_hi[:, :, D:768], wd[:, :, D:768]).then_inc(in_hi, 1)
            act.wait_ge(c_ld, 64)
            copy(identb[0:S, :], ident[0:S, 0:S])
            copy(maskb[0:S, :], maskf[0:S, :]).then_inc(const_done, 1)
            for r in range(2):
                for b in range(HB * r, HB * r + HB):
                    act.wait_ge(down_done, b + 1)
                    nc.scalar.activation(junk[0:S, b, 0:QR], ps[0:S, b, 0:QR], ACT.Square,
                                         scale=float(QR) ** -0.5, accum_out=ss[0:S, b, 0:1])
                    nc.scalar.activation(junk[0:S, b, QR:QR + LAT], ps[0:S, b, QR:QR + LAT], ACT.Square,
                                         scale=float(LAT) ** -0.5, accum_out=ss[0:S, b, 1:2])\
                        .then_inc(sq_done, 1)
                act.wait_ge(eps_done, r + 1)
                nc.scalar.activation(ss_root[0:S, HB * r:HB * r + HB, :],
                                     ss_eps[0:S, HB * r:HB * r + HB, :], ACT.Sqrt).then_inc(root_done, 1)
                if r == 1:
                    act.wait_ge(in_lo, 2 * KD + 2)
                    act.wait_ge(st_ld, 16)
                    for lo, hi in A_PIECES:
                        copy(wa_hi[:, lo:hi], stage[:, lo:hi]).then_inc(a_hi, 1)
                for b in range(HB * r, HB * r + HB):
                    act.wait_ge(nat_done, b + 1)
                    copy(kvN_hi[0:S, b, :], nat[0:S, b % 4, QR:QR + LAT]).then_inc(kvn_hi, 1)
                    act.wait_ge(tr_done, b + 1)
                    copy(qkT_hi[:, :, b * S:(b + 1) * S],
                         ps[:, b, 0:4 * S].rearrange("p (c s) -> p c s", c=4)).then_inc(tr_hi, 1)
            for half in range(2):
                act.wait_ge(kr_rot, half + 1)
                copy(kr_hi[:, half * HALF:(half + 1) * HALF], krt[:, 0, :]).then_inc(krh, 1)

            def layernorm_root(i, r):
                lo, hi = LN_PARTS[r]
                act.wait_ge(ln_eps, 2 * i + r + 1)
                nc.scalar.activation(rstd[:, lo:hi], rstd[:, lo:hi], ACT.Sqrt).then_inc(ln_root, 1)

            def turned(i, t, dst):
                act.wait_ge(lt_done, TT * i + t + 1)
                copy(dst[:, :, t * P:(t + 1) * P],
                     ps[:, t % 4, :].rearrange("p (c s) -> p c s", c=KD)).then_inc(lt_hi, 1)

            def split_l(g):
                act.wait_ge(st_ld, 32 * NG + 16 * g + 16)
                copy(wx_hi[:, 0:X_O], stage[:, 0:X_O]).then_inc(xl_hi, 1)

            def probabilities(m, b):
                act.wait_ge(max_done, m + 1)
                for h in range(GH):
                    last = nc.scalar.activation(Pt[0:S, b % 2, h * S:(h + 1) * S],
                                                ps[0:S, b % 2, h * S:(h + 1) * S], ACT.Exp,
                                                bias=negmax[0:S, b % 2, h:h + 1],
                                                accum_out=rowsum[0:S, b % 2, h:h + 1])
                last.then_inc(exp_done, 1)

            def transposed(m, b):
                act.wait_ge(pt_done, m + 1)
                copy(PT_hi[0:S, b % 2, :], ps[0:S, 2 + b % 2, 0:GH * S]).then_inc(pt_hi, 1)

            def att_step(item, g, at):
                kind, j = item[0], item[-1] if len(item) < 3 else item[1]
                if kind in ("A", "Q", "B"):
                    act.wait_ge(job_done, at.number + 1)
                    bank = ps[:, 6 + at.bank, :]
                    if kind == "A":
                        ins = copy(wa_hi[:, A_UP + j * D:A_UP + (j + 1) * D], bank, scale=ATT_SCALE)
                    elif kind == "B":
                        ins = copy(ws_hi[:, j * D:(j + 1) * D], bank)
                    else:
                        ins = copy(qa_hi[:, j, item[2] * HALF:(item[2] + 1) * HALF], bank[:, 0:HALF])
                    ins.then_inc(a_job_hi[kind], 1)
                elif kind == "G":
                    act.wait_ge(job_done, at.number + 1)
                    copy(sT[0:S, j % 2, :], ps[0:S, 6 + at.bank, 0:GH * S]).then_inc(a_free["G"], 1)
                elif kind == "R":
                    act.wait_ge(rot_add, 2 * g + j + 1)
                    act.wait_ge(pack_ld[1 - j], 16 + 256 * (g + j))
                    copy(ro_hi[:, :, :], rt[:, :, :]).then_inc(rot_hi, 1)
                elif kind == "SA":
                    lo, hi = A_PIECES[j]
                    act.wait_ge(st_ld, 32 * g + 16)
                    copy(wa_hi[:, lo:hi], stage[:, lo:hi]).then_inc(a_hi, 1)
                elif kind == "SB":
                    if j == 0:
                        act.wait_ge(st_ld, 32 * g + 32)
                        act.wait_ge(a_free["A"], AJ.count(("A", KQ - 1), g))
                    elif j == 1:
                        act.wait_ge(job_done, AJ.base(g))
                    copy(part_b(j, wa_hi, ws_hi), stage[:, slice(*B_PIECES[j])]).then_inc(bw_hi, 1)
                elif kind == "S":
                    probabilities(B * g + j, j)
                elif kind == "T":
                    transposed(B * g + j, j)
                elif kind == "Z":
                    act.wait_ge(z_done, B * g + j + 1)
                    copy(ZT_hi[:, :, j * S:(j + 1) * S],
                         ps[:, 4 + j % 2, 0:GH * S].rearrange("p (h s) -> p h s", h=GH))\
                        .then_inc(z_hi, 1)

                elif kind == "CX":
                    act.wait_ge(cx_ld, 16)
                    copy(cx_hi[:, :, :], cx[:, :, :]).then_inc(cxs_hi, 1)
                elif kind == "L":
                    split_l(0)
                elif kind == "LN1":
                    layernorm_root(0, j)
                elif kind == "U1":
                    turned(0, j, x1T_hi)

            turns(act.Fori, AJ, ATT_PRE, ATT_ACT, att_step)

            def x_step(item, g, at):
                kind, j = item[0], item[-1]
                m = NG * B + B * g
                if kind == "L":
                    split_l(g)
                elif kind == "X":
                    act.wait_ge(xo_ld, 16 * g + 16)
                    act.wait_ge(x_free["W"], 1 + TT * g)
                    copy(wx_hi[:, X_O:X_SIZE], stage[:, X_O:X_SIZE]).then_inc(xo_hi, 1)
                elif kind in ("Q", "K", "V"):
                    act.wait_ge(job_done, at.number + 1)
                    bank = ps[:, 6 + at.bank, :]
                    if kind == "Q":
                        ins = copy(qx_hi[:, j * HALF:(j + 1) * HALF], bank[:, 0:HALF], scale=X_SCALE)
                    elif kind == "V":
                        ins = copy(vN_hi[0:S, HB * j:HB * j + HB, :],
                                   bank[0:S, :].rearrange("p (b v) -> p b v", b=HB))
                    else:
                        act.wait_ge(kb_zero, 2)
                        for h in range(GH):
                            r = slice(DXH * h, DXH * (h + 1))
                            ins = copy(kb_hi[r, HB * j:HB * j + HB, h, :],
                                       bank[r, 0:HALF].rearrange("p (b s) -> p b s", b=HB))
                    ins.then_inc(x_job_hi[kind], 1)
                elif kind == "S":
                    probabilities(m + j, j)
                elif kind == "T":
                    transposed(m + j, j)
                elif kind == "Z":
                    act.wait_ge(z_done, m + j + 1)
                    for h in range(GH):
                        r = slice(DXH * h, DXH * (h + 1))
                        ins = copy(zx_hi[r, j * S:(j + 1) * S], ps[r, 4 + j % 2, h * S:(h + 1) * S])
                    ins.then_inc(z_hi, 1)

                elif kind == "U1":
                    turned(0, j, x1T_hi)
                elif kind == "LN2":
                    layernorm_root(1, j)
                elif kind == "U2":
                    turned(1, j, x2T_hi)
                elif kind == "F":
                    act.wait_ge(f_ld[j], 16)
                    copy(ws_hi[:, j * CHUNK:(j + 1) * CHUNK], stage[:, j * ROW:j * ROW + CHUNK])\
                        .then_inc(fw_hi, 1)
                elif kind == "G":
                    act.wait_ge(b_ld, 64)
                    copy(gw_hi[:, :, :], gw[:, :, :]).then_inc(g_hi, 1)
                    copy(e2_hi[:, :], e2[:, :]).then_inc(e_hi, 1)

            turns(act.Fori, XJ, X_PRE_ACT, X_ACT, x_step)
            for t in range(*LN_PARTS[1]):
                turned(1, t, x2T_hi)

            def up_tile(n, par, j, routed):
                for half in range(2):
                    q = 2 * FG * n + 2 * j + half
                    slot = (2 * j + half) % 4
                    cols = slice(half * HALF, (half + 1) * HALF)
                    act.wait_ge(up_done, q + 1)
                    act.wait_ge(h_lo_done, q + 1)
                    bias = b1[:, j:j + 1]
                    src = ps[:, slot, 0:HALF]
                    if routed is None:
                        nc.scalar.activation(hf[:, slot, :], src, ACT.Gelu, bias=bias)
                        nc.scalar.activation(h_hi[:, par, j, cols], src, ACT.Gelu, bias=bias)\
                            .then_inc(gelu_done, 1)
                    else:
                        nc.scalar.activation(hf[:, slot, :], src, ACT.Gelu, bias=bias)\
                            .then_inc(gelu_done, 1)
                        act.wait_ge(mix_done, 2 * FG * routed + 2 * j + half + 1)
                        copy(h_hi[:, par, j, cols], hf[:, slot, :]).then_inc(h_hi_done, 1)

            def stage_of(n, par, routed):
                for j in range(FG):
                    up_tile(n, par, j, routed)
                    s = j % 2
                    act.wait_ge(f_ld[s], 32 * n + 16 * (2 + j // 2))
                    if s == 0:
                        dst = w2_hi[:, par, j:j + 2, :].rearrange("p j n -> p (j n)")
                    else:
                        dst = ws_hi[:, (j - 1) * D:(j + 1) * D]
                    copy(dst, stage[:, s * ROW:s * ROW + CHUNK]).then_inc(fw_hi, 1)

            stage_of(0, 0, None)
            act.wait_ge(g_step, 3)
            nc.scalar.activation(gt[1][:, :, :], gt[1][:, :, :], ACT.Exp).then_inc(g_exp, 1)
            stage_of(1, 1, None)
            with act.Fori(0, (NSH - 2) // 2) as i:
                stage_of(2 * i + 2, 0, None)
                stage_of(2 * i + 3, 1, None)
            act.wait_ge(cT_ld, 16)
            act.wait_ge(e_one, 2)
            copy(cT_hi[0:E, :], cT_f[0:E, :]).then_inc(e_hi, 1)
            with act.Fori(0, (NF - NSH) // 2) as i:
                stage_of(2 * i + NSH, 0, 2 * i)
                stage_of(2 * i + NSH + 1, 1, 2 * i + 1)
            for t in range(TT):
                act.wait_ge(ln_eps, 4 + t + 1)
                nc.scalar.activation(rstd[:, t:t + 1], rstd[:, t:t + 1], ACT.Sqrt).then_inc(ln_root, 1)

        @block.vector
        def _(dve):
            def low(dst, src, hi, **kw):
                return nc.vector.tensor_tensor(dst, src, f32(hi), ALU.subtract)

            def low_scaled(dst, src, hi, scale):
                return nc.vector.scalar_tensor_tensor(dst, src, scale, f32(hi), ALU.mult, ALU.subtract)

            for s_, n in ((pt_free, 2), (z_free, 2), (fw_lo, 2), (h_lo_done, 4),
                          (y_free, 4), (cb_free, FG), (a_free["W"], 1), (x_free["W"], 1)):
                dve.sem_inc(s_, n)
            for k in range(KD):
                dve.wait_ge(in_hi, 2 * k + 1)
                low(wd_lo[:, k, 0:D], wd[:, k, 0:D], wd_hi[:, k, 0:D]).then_inc(in_lo, 1)
                dve.wait_ge(in_hi, 2 * k + 2)
                low(xT_lo[:, k, 0:HALF], xT[:, k, 0:HALF], xT_hi[:, k, 0:HALF]).then_inc(in_lo, 1)
            dve.wait_ge(in_hi, 2 * KD + 1)
            low(xT_lo[:, :, HALF:T], xT[:, :, HALF:T], xT_hi[:, :, HALF:T]).then_inc(in_lo, 1)
            dve.wait_ge(in_hi, 2 * KD + 2)
            low(wd_lo[:, :, D:768], wd[:, :, D:768], wd_hi[:, :, D:768]).then_inc(in_lo, 1)
            dve.wait_ge(c_ld, 64)
            for r in range(2):
                rows = slice(HB * r, HB * r + HB)
                dve.wait_ge(sq_done, HB * r + HB)
                nc.vector.tensor_scalar(ss_eps[0:S, rows, :], ss[0:S, rows, :], RMS_EPS, None, ALU.add)\
                  .then_inc(eps_done, 1)
                dve.wait_ge(root_done, r + 1)
                nc.vector.reciprocal(rinv[0:S, rows, :], ss_root[0:S, rows, :]).then_inc(rinv_done, 1)
                dve.wait_ge(rinv_done, r + 1)
                for b in range(HB * r, HB * r + HB):
                    if b >= 4:
                        dve.wait_ge(tr_done, b - 3)
                        dve.wait_ge(kvn_hi, b - 3)
                    for q, (lo, hi) in enumerate(((0, QR), (QR, QR + LAT))):
                        ins = nc.vector.scalar_tensor_tensor(nat[0:S, b % 4, lo:hi], ps[0:S, b, lo:hi],
                                                             rinv[0:S, b, q:q + 1], wnorm[0:S, lo:hi],
                                                             ALU.mult, ALU.mult)
                    ins.then_inc(nat_done, 1)
                for b in range(HB * r, HB * r + HB):
                    dve.wait_ge(kvn_hi, b + 1)
                    low(kvN_lo[0:S, b, :], nat[0:S, b % 4, QR:QR + LAT], kvN_hi[0:S, b, :])\
                        .then_inc(kvn_lo, 1)
                    dve.wait_ge(tr_hi, b + 1)
                    cols = slice(b * S, (b + 1) * S)
                    low(qkT_lo[:, :, cols], ps[:, b, 0:4 * S].rearrange("p (c s) -> p c s", c=4),
                        qkT_hi[:, :, cols]).then_inc(tr_lo, 1)

            def table(i):
                return tab[:, i, :].unsqueeze(1).broadcast_to([P, HB, S])

            def batches(ap):
                return ap.rearrange("p (b s) -> p b s", b=HB)

            for half in range(2):
                if half:
                    dve.wait_ge(krl, half)
                for s in range(2):
                    dve.wait_ge(kr_done, 2 * half + s + 1)
                    ins = nc.vector.tensor_tensor(batches(krt[:, s, :]),
                                                  batches(ps[:, 2 * half + s, 0:HALF]), table(2 + s),
                                                  ALU.mult)
                ins.then_inc(kr_mul, 1)
                dve.wait_ge(kr_mul, half + 1)
                nc.vector.tensor_tensor(krt[:, 0, :], krt[:, 0, :], krt[:, 1, :], ALU.add)\
                  .then_inc(kr_rot, 1)
                dve.wait_ge(krh, half + 1)
                cols = slice(half * HALF, (half + 1) * HALF)
                low(kr_lo[:, cols], krt[:, 0, :], kr_hi[:, cols]).then_inc(krl, 1)
            dve.wait_ge(acc_ld, 16)

            def row_max(m, b):
                dve.wait_ge(sc_done, m + 1)
                nc.vector.tensor_reduce(negmax[0:S, b % 2, :],
                                        ps[0:S, b % 2, 0:GH * S].rearrange("p (h k) -> p h k", h=GH),
                                        AX, ALU.max, negate=True).then_inc(max_done, 1)

            def row_inverse(m, b):
                dve.wait_ge(exp_done, m + 3)
                nc.vector.reciprocal(rowinv[0:S, b % 2, :], rowsum[0:S, b % 2, :]).then_inc(inv_done, 1)

            def transposed(m, b):
                dve.wait_ge(pt_hi, m + 1)
                low(PT_lo[0:S, b % 2, :], ps[0:S, 2 + b % 2, 0:GH * S], PT_hi[0:S, b % 2, :])\
                    .then_inc(pt_free, 1)

            def add_output(at, t, free):
                dve.wait_ge(job_done, at.number + 1)
                nc.vector.tensor_tensor(acc[:, t, :], ps[:, 6 + at.bank, :], acc[:, t, :], ALU.add)\
                  .then_inc(free, 1)

            def tile_stats(i, t, free):
                dve.wait_ge(free["W"], 1 + TT * (NG - 1) + t + 1)
                nc.vector.bn_stats(stats[:, t, :], acc[:, t, :]).then_inc(ln_stat, 1)

            def layernorm(i, r):
                lo, hi = LN_PARTS[r]
                dve.wait_ge(ln_stat, TT * i + hi)
                for t in range(lo, hi):
                    ins = nc.vector.bn_aggr(mv[:, t, :], stats[:, t, :])
                ins.then_inc(ln_mv, 1)
                dve.wait_ge(ln_mv, 2 * i + r + 1)
                nc.vector.tensor_scalar(rstd[:, lo:hi], mv[:, lo:hi, 1], LN_EPS, None, ALU.add)\
                  .then_inc(ln_eps, 1)
                dve.wait_ge(ln_root, 2 * i + r + 1)
                nc.vector.reciprocal(rstd[:, lo:hi], rstd[:, lo:hi]).then_inc(ln_inv, 1)
                dve.wait_ge(ln_inv, 2 * i + r + 1)
                for t in range(lo, hi):
                    nc.vector.tensor_scalar(acc[:, t, :], acc[:, t, :], mv[:, t, 0:1], rstd[:, t:t + 1],
                                            ALU.subtract, ALU.mult).then_inc(ln_out, 1)

            def turned(i, t, dst, hi):
                dve.wait_ge(lt_hi, TT * i + t + 1)
                cols = slice(t * P, (t + 1) * P)
                low(dst[:, :, cols], ps[:, t % 4, :].rearrange("p (c s) -> p c s", c=KD), hi[:, :, cols])\
                    .then_inc(lt_lo, 1)

            def att_step(item, g, at):
                kind, j = item[0], item[-1] if len(item) < 3 else item[1]
                m = B * g + j if kind in ("S", "N", "T", "Z") else None
                if kind in ("A", "Q", "B"):
                    dve.wait_ge(a_job_hi[kind], AJ.count(item, g))
                    bank = ps[:, 6 + at.bank, :]
                    if kind == "A":
                        cols = slice(A_UP + j * D, A_UP + (j + 1) * D)
                        ins = low_scaled(wa_lo[:, cols], bank, wa_hi[:, cols], ATT_SCALE)
                    elif kind == "B":
                        cols = slice(j * D, (j + 1) * D)
                        ins = low(ws_lo[:, cols], bank, ws_hi[:, cols])
                    else:
                        cols = slice(item[2] * HALF, (item[2] + 1) * HALF)
                        ins = low(qa_lo[:, j, cols], bank[:, 0:HALF], qa_hi[:, j, cols])
                    ins.then_inc(a_free[kind], 1)
                elif kind in "EO":
                    dst = rt if kind == "E" else ru
                    tabs = (0, 1) if kind == "E" else (1, 0)
                    dve.wait_ge(job_done, at.number + 1)
                    if kind == "E":
                        dve.wait_ge(rot_lo, 2 * g + j + 1)
                    for i in range(2):
                        ins = nc.vector.tensor_tensor(batches(dst[:, i, :]),
                                                      batches(ps[:, 6 + at.bank, 0:HALF]),
                                                      table(tabs[i]), ALU.mult)
                    ins.then_inc(a_free[kind], 1)
                elif kind == "SA":
                    lo, hi = A_PIECES[j]
                    dve.wait_ge(a_hi, len(A_PIECES) * g + j + 1)
                    low(wa_lo[:, lo:hi], stage[:, lo:hi], wa_hi[:, lo:hi]).then_inc(a_lo, 1)
                elif kind == "SB":
                    dve.wait_ge(bw_hi, len(B_PIECES) * g + j + 1)
                    low(part_b(j, wa_lo, ws_lo), stage[:, slice(*B_PIECES[j])],
                        part_b(j, wa_hi, ws_hi)).then_inc(bw_lo, 1)
                elif kind == "S":
                    row_max(m, j)
                elif kind == "N":
                    row_inverse(m, j)
                elif kind == "T":
                    transposed(m, j)
                elif kind == "Z":
                    dve.wait_ge(z_hi, m + 1)
                    cols = slice(j * S, (j + 1) * S)
                    low(ZT_lo[:, :, cols], ps[:, 4 + j % 2, 0:GH * S].rearrange("p (h s) -> p h s", h=GH),
                        ZT_hi[:, :, cols]).then_inc(z_free, 1)
                elif kind == "W":
                    add_output(at, j, a_free["W"])
                    if isinstance(g, int):
                        tile_stats(0, j, a_free)
                elif kind == "LN1":
                    layernorm(0, j)
                elif kind == "U1":
                    turned(0, j, x1T_lo, x1T_hi)

            turns(dve.Fori, AJ, ATT_PRE, ATT_DVE, att_step)

            def x_step(item, g, at):
                kind, j = item[0], item[-1]
                m = NG * B + B * g
                if kind in ("Q", "K", "V"):
                    dve.wait_ge(x_job_hi[kind], XJ.count(item, g))
                    bank = ps[:, 6 + at.bank, :]
                    bs = slice(HB * j, HB * j + HB)
                    if kind == "Q":
                        cols = slice(j * HALF, (j + 1) * HALF)
                        ins = low_scaled(qx_lo[:, cols], bank[:, 0:HALF], qx_hi[:, cols], X_SCALE)
                    elif kind == "V":
                        ins = low(vN_lo[0:S, bs, :], bank[0:S, :].rearrange("p (b v) -> p b v", b=HB),
                                  vN_hi[0:S, bs, :])
                    else:
                        for h in range(GH):
                            r = slice(DXH * h, DXH * (h + 1))
                            ins = low(kb_lo[r, bs, h, :],
                                      bank[r, 0:HALF].rearrange("p (b s) -> p b s", b=HB),
                                      kb_hi[r, bs, h, :])
                    ins.then_inc(x_free[kind], 1)
                elif kind == "S":
                    row_max(m + j, j)
                elif kind == "N":
                    row_inverse(m + j, j)
                elif kind == "T":
                    transposed(m + j, j)
                elif kind == "Z":
                    dve.wait_ge(z_hi, m + j + 1)
                    cols = slice(j * S, (j + 1) * S)
                    for h in range(GH):
                        r = slice(DXH * h, DXH * (h + 1))
                        ins = low(zx_lo[r, cols], ps[r, 4 + j % 2, h * S:(h + 1) * S], zx_hi[r, cols])
                    ins.then_inc(z_free, 1)
                elif kind == "W":
                    add_output(at, j, x_free["W"])
                    if isinstance(g, int):
                        tile_stats(1, j, x_free)
                elif kind == "U1":
                    turned(0, j, x1T_lo, x1T_hi)
                elif kind == "LN2":
                    layernorm(1, j)
                elif kind == "U2":
                    turned(1, j, x2T_lo, x2T_hi)
                elif kind == "F":
                    dve.wait_ge(fw_hi, j + 1)
                    cols = slice(j * CHUNK, (j + 1) * CHUNK)
                    nc.vector.tensor_copy(b1[:, 2 * j:2 * j + 2], stage[:, j * ROW + CHUNK:(j + 1) * ROW])
                    low(ws_lo[:, cols], stage[:, j * ROW:j * ROW + CHUNK], ws_hi[:, cols]).then_inc(fw_lo, 1)
                elif kind == "G":
                    dve.wait_ge(g_hi, 1)
                    low(gw_lo[:, :, :], gw[:, :, :], gw_hi[:, :, :]).then_inc(g_lo, 1)
                    dve.wait_ge(e_hi, 1)
                    low(e2_lo[:, :], e2[:, :], e2_hi[:, :]).then_inc(e_lo, 1)

            turns(dve.Fori, XJ, X_PRE_DVE, X_DVE, x_step)
            for t in range(*LN_PARTS[1]):
                turned(1, t, x2T_lo, x2T_hi)

            step = [0]

            def then(ins):
                step[0] += 1
                ins.then_inc(g_step, 1)
                dve.wait_ge(g_step, step[0])

            def wide(ap):
                return ap.unsqueeze(2).broadcast_to([P, TT, E])

            def per_expert(ap):
                return ap[:, :].unsqueeze(1).broadcast_to([P, TT, E])

            def gates():
                V = nc.vector
                dve.wait_ge(g_done, 1)
                logits, soft, eq1, sel1, rest, eq2, sel2, both_, mix = gt
                then(V.tensor_tensor(logits[:, :, :], ps[:, 7, 0:TT * E].rearrange("p (t e) -> p t e", t=TT),
                                     per_expert(gb), ALU.add))
                then(V.tensor_reduce(g1[:, 0, :], logits[:, :, :], AX, ALU.max))
                then(V.tensor_tensor(soft[:, :, :], logits[:, :, :], wide(g1[:, 0, :]), ALU.subtract))
                dve.wait_ge(g_exp, 1)
                then(V.tensor_reduce(g1[:, 1, :], soft[:, :, :], AX, ALU.add))
                then(V.reciprocal(g1[:, 2, :], g1[:, 1, :]))
                then(V.tensor_tensor(soft[:, :, :], soft[:, :, :], wide(g1[:, 2, :]), ALU.mult))
                left = soft
                for k, (eq, sel) in enumerate(((eq1, sel1), (eq2, sel2))):
                    then(V.tensor_reduce(g1[:, 3, :], left[:, :, :], AX, ALU.max))
                    then(V.tensor_tensor(eq[:, :, :], left[:, :, :], wide(g1[:, 3, :]), ALU.is_equal))
                    then(V.tensor_tensor(eq[:, :, :], eq[:, :, :], per_expert(rev), ALU.mult))
                    then(V.tensor_reduce(g1[:, 4, :], eq[:, :, :], AX, ALU.max))
                    then(V.tensor_tensor(sel[:, :, :], eq[:, :, :], wide(g1[:, 4, :]), ALU.is_equal))
                    if k == 0:
                        then(V.scalar_tensor_tensor(rest[:, :, :], sel[:, :, :], -4.0, soft[:, :, :],
                                                    ALU.mult, ALU.add))
                        left = rest
                then(V.tensor_tensor(both_[:, :, :], sel1[:, :, :], sel2[:, :, :], ALU.add))
                V.tensor_tensor(mix[:, :, :], both_[:, :, :], soft[:, :, :], ALU.mult).then_inc(g_mix, 1)

            def up_tile(n, par, j, routed):
                for half in range(2):
                    q = 2 * FG * n + 2 * j + half
                    slot = (2 * j + half) % 4
                    cols = slice(half * HALF, (half + 1) * HALF)
                    dve.wait_ge(gelu_done, q + 5)
                    if routed is not None:
                        if half == 0:
                            dve.wait_ge(cb_ld[j], 16 * routed + 16)
                        ins = nc.vector.tensor_tensor(hf[:, slot, :], hf[:, slot, :], cb[:, j, cols],
                                                      ALU.mult)
                        ins.then_inc(mix_done, 1)
                        dve.wait_ge(h_hi_done, 2 * FG * routed + 2 * j + half + 1)
                        if half == 1:
                            dve.sem_inc(cb_free, 1)
                    low(h_lo[:, par, j, cols], hf[:, slot, :], h_hi[:, par, j, cols])\
                        .then_inc(h_lo_done, 1)

            def down_tile(n, t):
                dve.wait_ge(y_done, TT * n + t + 1)
                nc.vector.tensor_tensor(acc[:, t, :], ps[:, 4 + t % 4, :], acc[:, t, :], ALU.add)\
                  .then_inc(y_free, 1)

            def stage_of(n, par, routed, down=True):
                tiles = [(0, 1), (2, 3), (4, 5), (6,)]
                for j in range(FG):
                    up_tile(n, par, j, routed)
                    if isinstance(n, int) and n == 0 and j == 0:
                        for half in range(2):
                            dve.wait_ge(g_log, half + 1)
                            nc.vector.tensor_copy(lg[:, half * HALF:(half + 1) * HALF],
                                                  ps[0:E, 4 + half, 0:HALF]).then_inc(g_lg, 1)
                    if isinstance(n, int) and n == 1 and j == 1:
                        dve.wait_ge(g_tr, 1)
                        nc.vector.tensor_copy(ct[:, :], ps[0:TT * E, 7, 0:P]).then_inc(g_ct, 1)
                    if down:
                        for t in tiles[j]:
                            down_tile(n - 1, t)
                    s = j % 2
                    dve.wait_ge(fw_hi, 4 * n + 3 + j)
                    if s == 0:
                        dst, hi = (x[:, par, j:j + 2, :].rearrange("p j n -> p (j n)") for x in (w2_lo, w2_hi))
                    else:
                        dst, hi = (x[:, (j - 1) * D:(j + 1) * D] for x in (ws_lo, ws_hi))
                        nc.vector.tensor_copy(b1[:, j - 1:j + 1], stage[:, s * ROW + CHUNK:(s + 1) * ROW])
                    low(dst, stage[:, s * ROW:s * ROW + CHUNK], hi).then_inc(fw_lo, 1)

            stage_of(0, 0, None, down=False)
            gates()
            stage_of(1, 1, None)
            with dve.Fori(0, (NSH - 2) // 2) as i:
                stage_of(2 * i + 2, 0, None)
                stage_of(2 * i + 3, 1, None)
            dve.wait_ge(e_hi, 2)
            low(cT_lo[0:E, :], cT_f[0:E, :], cT_hi[0:E, :]).then_inc(e_lo, 1)
            with dve.Fori(0, (NF - NSH) // 2) as i:
                stage_of(2 * i + NSH, 0, 2 * i)
                stage_of(2 * i + NSH + 1, 1, 2 * i + 1)
            for t in range(TT):
                down_tile(NF - 1, t)
                dve.wait_ge(y_free, 4 + TT * (NF - 1) + t + 1)
                nc.vector.bn_stats(stats[:, t, :], acc[:, t, :]).then_inc(ln_stat, 1)
                dve.wait_ge(ln_stat, 2 * TT + t + 1)
                nc.vector.bn_aggr(mv[:, t, :], stats[:, t, :]).then_inc(ln_mv, 1)
                dve.wait_ge(ln_mv, 4 + t + 1)
                nc.vector.tensor_scalar(rstd[:, t:t + 1], mv[:, t, 1:2], LN_EPS, None, ALU.add)\
                  .then_inc(ln_eps, 1)
                dve.wait_ge(ln_root, 4 + t + 1)
                nc.vector.reciprocal(rstd[:, t:t + 1], rstd[:, t:t + 1]).then_inc(ln_inv, 1)
                dve.wait_ge(ln_inv, 4 + t + 1)
                nc.vector.tensor_scalar(acc[:, t, :], acc[:, t, :], mv[:, t, 0:1], rstd[:, t:t + 1],
                                        ALU.subtract, ALU.mult).then_inc(ln_out, 1)

        @block.tensor
        def _(pe):
            mm = nc.tensor.matmul

            def product(dst, terms, start=True, stop=True):
                ops = [p for w, x in terms for p in three(w, x)]
                for i, (w, x) in enumerate(ops):
                    ins = mm(dst, w, x, start=start and i == 0, stop=stop and i == len(ops) - 1,
                             skip_group_check=not (start and stop))
                return ins

            def two(hl, *idx):
                return tuple(x[idx] for x in hl)

            for r in range(2):
                for k in range(KD):
                    pe.wait_ge(in_lo, 2 * k + 2 if r == 0 else 2 * KD + 1)
                    for b in range(HB * r, HB * r + HB):
                        ops = three(two((xT_hi, xT_lo), slice(None), k, slice(b * S, (b + 1) * S)),
                                    two((wd_hi, wd_lo), slice(None), k, slice(0, D)))
                        for i, (w, x) in enumerate(ops):
                            ins = mm(ps[0:S, b, :], w, x, start=k == 0 and i == 0,
                                     stop=k == KD - 1 and i == 2)
                        if k == KD - 1:
                            ins.then_inc(down_done, 1)

            def turn_latents(b):
                pe.wait_ge(nat_done, b + 1)
                for c in range(4):
                    ins = nc.tensor.transpose(ps[:, b, c * S:(c + 1) * S], nat[0:S, b % 4, c * P:(c + 1) * P],
                                              ident[0:S, 0:S])
                ins.then_inc(tr_done, 1)

            for b in range(HB):
                turn_latents(b)
            pe.wait_ge(in_lo, 2 * KD + 2)
            for half in range(2):
                for s in range(2):
                    bank = 2 * half + s
                    pe.wait_ge(tr_lo, bank + 1)
                    cols = slice(half * HALF, (half + 1) * HALF)
                    product(ps[:, bank, 0:HALF],
                            [(two((wd_hi, wd_lo), slice(None), k, slice(D + P * s, D + P * s + P)),
                              two((xT_hi, xT_lo), slice(None), k, cols)) for k in range(KD)])\
                        .then_inc(kr_done, 1)
                if half == 0:
                    for b in range(HB, B):
                        turn_latents(b)
            pe.wait_ge(tr_lo, B)

            def heads(ap):
                return ap.rearrange("p (h s) -> p h s", h=GH)

            def mask(dst, w, x):
                mm(heads(dst), w[0:S, :], x[0:S, :].unsqueeze(1).broadcast_to([S, GH, S]), start=True,
                   stop=False, skip_group_check=True)

            def transposes(m, b):
                pe.wait_ge(norm_done, m + 1)
                pe.wait_ge(pt_free, m + 1)
                for h in range(GH):
                    ins = nc.tensor.transpose(ps[0:S, 2 + b % 2, h * S:(h + 1) * S],
                                              Pt[0:S, b % 2, h * S:(h + 1) * S], ident[0:S, 0:S])
                ins.then_inc(pt_done, 1)

            def weigh(m, b, w):
                pe.wait_ge(pt_free, m + 3)
                pe.wait_ge(z_free, m + 1)
                product(ps[:, 4 + b % 2, 0:GH * S],
                        [(w, two((PT_hi, PT_lo), slice(0, S), b % 2, slice(None)))]).then_inc(z_done, 1)

            def bank_free(free, at):
                if at and at.prev:
                    pe.wait_ge(free[at.prev[0]], at.prev_count + (at.prev[0] == "W"))

            def turn(i, t):
                pe.wait_ge(ln_out, TT * i + t + 1)
                if t >= 4:
                    pe.wait_ge(lt_lo, TT * i + t - 3)
                for c in range(KD):
                    ins = nc.tensor.transpose(ps[:, t % 4, c * P:(c + 1) * P], acc[:, t, c * P:(c + 1) * P],
                                              ident[:, :])
                ins.then_inc(lt_done, 1)

            def keys_ready():
                pe.wait_ge(kvn_lo, B)
                pe.wait_ge(krl, 2)
                pe.wait_ge(const_done, 1)

            def att_step(item, g, at):
                kind, j = item[0], item[-1] if len(item) < 3 else item[1]
                if at:
                    bank_free(a_free, at)
                    bank = ps[:, 6 + at.bank, :]
                if kind in "EO":
                    pe.wait_ge(a_lo, len(A_PIECES) * g + 1)
                    off = A_ROPE + (0 if kind == "E" else P)
                    cols = slice(j * HALF, (j + 1) * HALF)
                    ins = product(bank[:, 0:HALF],
                                  [(two(wa, slice(None), slice(off + 256 * c, off + 256 * c + P)),
                                    two((qkT_hi, qkT_lo), slice(None), c, cols)) for c in range(KQ)])
                elif kind == "A":
                    pe.wait_ge(a_lo, len(A_PIECES) * (g + 1))
                    for h in range(GH):
                        u, k = A_UP + j * D + h * P, A_K + h * LAT
                        ins = product(bank[:, h * LAT:(h + 1) * LAT],
                                      [(two(wa, slice(None), slice(u, u + P)),
                                        two(wa, slice(None), slice(k, k + LAT)))])
                elif kind == "Q":
                    pe.wait_ge(a_free["A"], AJ.count(("A", KQ - 1), g))
                    cols = slice(item[2] * HALF, (item[2] + 1) * HALF)
                    ins = product(bank[:, 0:HALF],
                                  [(two(wa, slice(None), slice(A_UP + c * D + j * LAT,
                                                               A_UP + c * D + (j + 1) * LAT)),
                                    two((qkT_hi, qkT_lo), slice(None), c, cols)) for c in range(KQ)])
                elif kind == "B":
                    pe.wait_ge(bw_lo, len(B_PIECES) * g + (2 if j < 2 else 3))
                    v = A_K + j * LAT
                    ins = product(bank, [(two(wa, slice(None), slice(v, v + LAT)),
                                          two(ws, slice(None), slice(j * D, (j + 1) * D)))])
                elif kind == "W":
                    pe.wait_ge(z_free, 2 + B * g + last_batch(j) + 1)
                    pe.wait_ge(a_free["B"], AJ.count(("B", GH - 1), g))
                    ins = product(bank, [(two((ZT_hi, ZT_lo), slice(None), h, slice(j * P, (j + 1) * P)),
                                          two(ws, slice(None), slice(h * D, (h + 1) * D)))
                                         for h in range(GH)])
                elif kind == "G":
                    if isinstance(g, int) and g == 0 and j == 0:
                        keys_ready()
                    pe.wait_ge(a_free["Q"], AJ.count(("Q", GH - 1, j // HB), g))
                    pe.wait_ge(pack_ld[j // HB], 16 + 256 * (g + 1))
                    tok = slice(j * S, (j + 1) * S)
                    mask(bank[0:S, 0:GH * S], maskb, identb)
                    ops = three(two((qkT_hi, qkT_lo), slice(None), KQ, tok),
                                two((qa_hi, qa_lo), slice(None), slice(None), tok))
                    ops += tuple((k[:, tok], qr[:, :, tok]) for k in (kr_hi, kr_lo))
                    for i, (w, x) in enumerate(ops):
                        ins = mm(heads(bank[0:S, 0:GH * S]), w, x, start=False, stop=i == len(ops) - 1,
                                 skip_group_check=True)
                if at:
                    ins.then_inc(job_done, 1)
                if kind == "S":
                    pe.wait_ge(exp_done, B * g + j + 1)
                    pe.wait_ge(a_free["G"], AJ.count(("G", j), g))
                    for h in range(GH):
                        ins = nc.tensor.transpose(ps[0:S, j % 2, h * S:(h + 1) * S],
                                                  sT[0:S, j % 2, h * S:(h + 1) * S], ident[0:S, 0:S])
                    ins.then_inc(sc_done, 1)
                elif kind == "T":
                    transposes(B * g + j, j)
                elif kind == "Z":
                    weigh(B * g + j, j, two((kvN_hi, kvN_lo), slice(0, S), j, slice(None)))
                elif kind == "U1":
                    turn(0, j)

            def att_ready():
                for item in AJ.pre[-2:]:
                    pe.wait_ge(a_free[item[0]], AJ.count(item, 0))

            turns(pe.Fori, AJ, ATT_PRE, ATT_PE, att_step, att_ready)

            pe.wait_ge(a_free["W"], 1 + NG * TT)

            def x_step(item, g, at):
                kind, j = item[0], item[-1]
                m = NG * B + B * g
                if at:
                    bank_free(x_free, at)
                    bank = ps[:, 6 + at.bank, :]
                if kind in ("Q", "K", "V"):
                    pe.wait_ge(xl_lo, g + 1)
                    pe.wait_ge(cxs_lo, 1)
                    cols = slice(j * HALF, (j + 1) * HALF)
                    ctx_half = tuple(x[:, HB * j:HB * j + HB, :].rearrange("p b s -> p (b s)")
                                     for x in (cx_hi, cx_lo))
                if kind == "Q":
                    pe.wait_ge(lt_lo, (4, TT)[j])
                    ins = product(bank[:, 0:HALF],
                                  [(two(wx, slice(None), slice(X_Q + P * k, X_Q + P * k + P)),
                                    two((x1T_hi, x1T_lo), slice(None), k, cols)) for k in range(KD)])
                elif kind == "K":
                    ins = product(bank[:, 0:HALF], [(two(wx, slice(None), slice(X_K, X_K + P)), ctx_half)])
                elif kind == "V":
                    for b in range(HB):
                        ins = product(bank[0:S, b * P:(b + 1) * P],
                                      [(two((cx_hi, cx_lo), slice(None), HB * j + b, slice(None)),
                                        two(wx, slice(None), slice(X_V, X_V + P)))])
                elif kind == "W":
                    pe.wait_ge(z_free, 2 + m + last_batch(j) + 1)
                    pe.wait_ge(xo_lo, g + 1)
                    ins = product(bank, [(two((zx_hi, zx_lo), slice(None), slice(j * P, (j + 1) * P)),
                                          two(wx, slice(None), slice(X_O, X_O + D)))])
                if at:
                    ins.then_inc(job_done, 1)
                if kind == "S":
                    if isinstance(g, int) and j == 0:
                        pe.wait_ge(lt_lo, TT)
                    pe.wait_ge(exp_done, m + j + 1)
                    pe.wait_ge(x_free["K"], XJ.count(("K", j // HB), g))
                    pe.wait_ge(x_free["Q"], XJ.count(("Q", j // HB), g))
                    mask(ps[0:S, j % 2, 0:GH * S], identb, maskb)
                    keys = tuple(x[:, j, :, :].rearrange("p h s -> p (h s)") for x in (kb_hi, kb_lo))
                    ops = three(two((qx_hi, qx_lo), slice(None), slice(j * S, (j + 1) * S)), keys)
                    for i, (w, x) in enumerate(ops):
                        ins = mm(ps[0:S, j % 2, 0:GH * S], w, x, start=False, stop=i == 2,
                                 skip_group_check=True)
                    ins.then_inc(sc_done, 1)
                elif kind == "T":
                    transposes(m + j, j)
                elif kind == "Z":
                    pe.wait_ge(x_free["V"], XJ.count(("V", j // HB), g))
                    weigh(m + j, j, two((vN_hi, vN_lo), slice(0, S), j, slice(None)))
                elif kind == "U1":
                    turn(0, j)
                elif kind == "U2":
                    turn(1, j)

            def x_ready():
                for item in XJ.pre[-2:]:
                    pe.wait_ge(x_free[item[0]], XJ.count(item, 0))

            turns(pe.Fori, XJ, X_PRE_PE, X_PE, x_step, x_ready)

            def logits(half):
                pe.wait_ge(g_lo, 1)
                if half == 0:
                    pe.wait_ge(z_free, 2 + 2 * NG * B)
                for k in range(KD):
                    w = two((gw_hi, gw_lo), slice(None), k, slice(None))
                    x = two((x2T_hi, x2T_lo), slice(None), k, slice(half * HALF, (half + 1) * HALF))
                    ops = [(a, b_) for a in w for b_ in x]
                    for i, (a, b_) in enumerate(ops):
                        ins = mm(ps[0:E, 4 + half, 0:HALF], a, b_, start=k == 0 and i == 0,
                                 stop=k == KD - 1 and i == len(ops) - 1)
                ins.then_inc(g_log, 1)

            def logits_turned():
                pe.wait_ge(g_lg, 2)
                pe.wait_ge(x_free["W"], 1 + NG * TT)
                for t in range(TT):
                    ins = nc.tensor.transpose(ps[:, 7, t * E:(t + 1) * E], lg[:, t * P:(t + 1) * P],
                                              ident[0:E, 0:E])
                ins.then_inc(g_done, 1)

            def up_tile(n, j):
                first = isinstance(n, int) and n == 0
                chunk = j // 2 if first else 4 * n - 1 + 2 * (j // 2)
                pe.wait_ge(fw_lo, 2 + chunk + 1)
                for half in range(2):
                    q = 2 * FG * n + 2 * j + half
                    pe.wait_ge(gelu_done, q + 1)
                    if first and j == 0:
                        pe.wait_ge(lt_lo, TT + (5, TT)[half])
                    product(ps[:, (2 * j + half) % 4, 0:HALF],
                            [(two(ws, slice(None), slice(D * j + P * k, D * j + P * k + P)),
                              two((x2T_hi, x2T_lo), slice(None), k, slice(half * HALF, (half + 1) * HALF)))
                             for k in range(KD)]).then_inc(up_done, 1)
                    if first and j == 0:
                        if half == 0:
                            for t in range(*LN_PARTS[1]):
                                turn(1, t)
                        logits(half)
                if first and j == 2:
                    logits_turned()

            def down_tile(n, par, t, biases=False):
                if t == 0:
                    pe.wait_ge(h_lo_done, 4 + 2 * FG * n + 2 * FG)
                    pe.wait_ge(fw_lo, 2 + 4 * n + 5)
                pe.wait_ge(y_free, TT * n + t + (2 if t < 3 else 1))
                tok = slice(t * P, (t + 1) * P)
                dst = ps[:, 4 + t % 4, :]
                if biases:
                    product(dst, [(two((cT_hi, cT_lo), slice(None), tok), two((e2_hi, e2_lo), slice(None), slice(None)))],
                            stop=False)
                product(dst, [(two((h_hi, h_lo), slice(None), par, j, tok),
                               two((w2_hi, w2_lo), slice(None), par, j, slice(None))) for j in range(FG)],
                        start=not biases).then_inc(y_done, 1)

            def stage_of(n, par, down=True):
                tiles = [(0, 1), (2, 3), (4, 5), (6,)]
                for j in range(FG):
                    up_tile(n, j)
                    if isinstance(n, int) and n == 1 and j == 1:
                        pe.wait_ge(g_mix, 1)
                        nc.tensor.transpose(ps[0:TT * E, 7, 0:P], gt[8][:, :, :].rearrange("p t e -> p (t e)"),
                                            ident[:, :]).then_inc(g_tr, 1)
                    if down:
                        for t in tiles[j]:
                            if isinstance(n, int) and t == 3:
                                pe.wait_ge(g_ct, 1)
                            down_tile(n - 1, 1 - par, t)

            stage_of(0, 0, down=False)
            stage_of(1, 1)
            with pe.Fori(0, (NSH - 2) // 2) as i:
                stage_of(2 * i + 2, 0)
                stage_of(2 * i + 3, 1)
            with pe.Fori(0, (NF - NSH) // 2) as i:
                stage_of(2 * i + NSH, 0)
                stage_of(2 * i + NSH + 1, 1)
            pe.wait_ge(e_lo, 2)
            for t in range(TT):
                down_tile(NF - 1, 1, t, biases=True)


def layouts(inputs):
    import numpy as np

    def a(name):
        return np.asarray(inputs[name])

    o = {}
    x = a("x").reshape(T, D)
    o["xT"] = x.T.reshape(KD, P, T).transpose(1, 0, 2)
    o["xN"] = x.reshape(TT, P, D).transpose(1, 0, 2)
    o["ctxT"] = a("ctx_512").transpose(2, 0, 1)
    kr = a("L0_attn_wk_rope")
    x1, x2 = kr[0::2], kr[1::2]
    down = np.concatenate([a("L0_attn_wq_down"), a("L0_attn_wkv_down"), x1, x2, x1, x2, x2, x1, x2, x1])
    o["wdown"] = down.T.reshape(KD, P, 768).transpose(1, 0, 2)
    o["wnorm"] = np.broadcast_to(np.concatenate([a("L0_attn_q_norm_w"), a("L0_attn_kv_norm_w")]), (P, D))
    rope = a("L0_attn_wq_rope").reshape(NG, GH, DR // 2, 2, KQ, P).transpose(0, 5, 4, 3, 1, 2)
    up = a("L0_attn_wq_up").reshape(NG, GH, DN, KQ, P).transpose(0, 2, 3, 1, 4)
    kv = a("L0_attn_wkv_up").reshape(NG, GH, 2, DN, LAT).transpose(2, 0, 3, 1, 4)
    wo = a("L0_attn_wo").reshape(D, NG, GH, DN).transpose(1, 3, 2, 0)
    flat = lambda z: z.reshape(NG, P, -1)
    o["wa"] = np.concatenate([flat(rope), flat(up), flat(kv[0])], axis=2)
    o["wb"] = np.concatenate([flat(kv[1]), flat(wo)], axis=2)
    wq = a("L0_xattn_Wq").reshape(NG, P, KD, P).transpose(0, 3, 2, 1)
    wk, wv = a("L0_xattn_Wkv_expand").reshape(2, NG, P, P).transpose(0, 1, 3, 2)
    wout = a("L0_xattn_Wout").reshape(D, NG, P).transpose(1, 2, 0)
    o["wx"] = np.concatenate([flat(wq), flat(wk), flat(wv), flat(wout)], axis=2)
    w1s = a("L0_ffn_sw1").reshape(2, KD, P, 16, P).transpose(0, 3, 2, 1, 4).reshape(32, P, D)
    w1e = a("L0_ffn_ew1").reshape(E, KD, P, P).transpose(0, 2, 1, 3).reshape(E, P, D)
    w1 = np.concatenate([w1s, w1e])
    w2 = np.concatenate([a("L0_ffn_sw2").reshape(32, P, D), a("L0_ffn_ew2")])
    pairs = lambda w: w.reshape(HT // 2, 2, P, D).transpose(0, 2, 1, 3).reshape(HT // 2, P, CHUNK)
    b1 = np.concatenate([a("L0_ffn_sb1").reshape(32, P), a("L0_ffn_eb1")])
    none = np.zeros((HT // 2, P, 2), np.float32)
    w1 = np.concatenate([pairs(w1), b1.reshape(HT // 2, 2, P).transpose(0, 2, 1)], axis=2)
    w2 = np.concatenate([pairs(w2), none], axis=2)
    order = [w1[0], w1[1]]
    for n in range(NF):
        last = n == NF - 1
        order += [w2[2 * n], np.zeros_like(w1[0]) if last else w1[2 * n + 2],
                  w2[2 * n + 1], np.zeros_like(w1[0]) if last else w1[2 * n + 3]]
    o["wf"] = np.stack(order)
    o["gw"] = a("L0_ffn_gate_w").reshape(KD, P, E).transpose(1, 0, 2)
    o["gb"] = np.broadcast_to(a("L0_ffn_gate_b"), (P, E))
    o["e2"] = np.concatenate([a("L0_ffn_eb2"), a("L0_ffn_sb2")])
    f = np.float32
    inv = (f(1.0) / f(10000.0) ** (np.arange(0, DR, 2, dtype=f) / f(DR))).astype(f)
    ang = np.outer(np.arange(S, dtype=f), inv).astype(f)
    c, s = np.tile(np.cos(ang).T, (4, 1)), np.tile(np.sin(ang).T, (4, 1))
    sign = np.repeat(np.array([-1, 1, -1, 1], f), 32)[:, None]
    o["tab"] = np.stack([c * f(ATT_SCALE), s * f(ATT_SCALE), c, s * sign], axis=1)
    o["ident"] = np.eye(P, dtype=f)
    o["mask"] = np.where(np.arange(P)[:, None] < np.arange(S), f(-3.0e38), f(0))
    o["rev"] = np.broadcast_to((E - np.arange(E)).astype(f), (P, E))
    return {k: np.ascontiguousarray(v) for k, v in o.items()}


def kernel(**inputs):
    import concourse.bacc as bacc
    from concourse.bass_utils import run_bass_kernel_spmd

    nc = bacc.Bacc("TRN2", target_bir_lowering=False, num_devices=1)
    arrays = layouts(inputs)
    d = {k: nc.dram_tensor(f"in_{k}", v.shape, F32, kind="ExternalInput").ap() for k, v in arrays.items()}
    scratch = nc.dram_tensor("mix_scratch", (E, T), F32, kind="Internal").ap()
    out = nc.dram_tensor("out", (T, D), F32, kind="ExternalOutput").ap()
    build(nc, d, scratch, out.rearrange("(t p) n -> p t n", p=P))
    r = run_bass_kernel_spmd(nc, [{f"in_{k}": v for k, v in arrays.items()}], core_ids=[0])
    return r.results[0]["out"].reshape(B, S, D)
```
